# Optimizing a Trainium2 kernel written in Bass

```python
import numpy as np
import jax
import jax.numpy as jnp

def _softmax(x, axis=-1):
    return jax.nn.softmax(x, axis=axis)

def _gelu(x):
    return jax.nn.gelu(x, approximate=True)

def _silu(x):
    return jax.nn.silu(x)

def _sigmoid(x):
    return jax.nn.sigmoid(x)

def _layernorm(x, axis=-1, eps=1e-05):
    m = jnp.mean(x, axis=axis, keepdims=True)
    v = jnp.var(x, axis=axis, keepdims=True)
    return (x - m) / jnp.sqrt(v + eps)

def _scatter_add(tgt, idx, src, axis=0):
    return tgt.at[idx].add(src)

def _segment_sum(src, seg, n):
    return jax.ops.segment_sum(src, seg, n)
kernel_name = 'mk_dlrm_tower_d1_rec_r8_bb2771'

def setup_inputs(seed: int=0):
    np.random.seed(seed)
    _w = jnp.asarray

    def _rec_inputs():
        import jax
        import jax.numpy as jnp
        _tk = jax.random.key(seed)
        dense_ctx = jax.random.normal(jax.random.fold_in(_tk, 190), (512, 16), jnp.float32)
        ids = jnp.stack([jax.random.randint(jax.random.fold_in(_tk, 200 + f), (512,), 0, v, jnp.int32) for f, v in enumerate([1000, 1000, 1250, 1000, 1250, 12500, 12500, 1250, 125000, 1000, 125000, 12500, 12500, 125000, 1250, 1000, 125000, 1250, 12500, 1250, 125000, 1000, 12500, 125000, 1000, 1000, 12500, 12500, 1250, 12500, 12500, 12500, 125000, 12500, 1250, 125000, 1000, 1250, 12500])], axis=1)
        tbl_0 = 0.05 * jax.random.normal(jax.random.fold_in(_tk, 500 + 0), (1000, 16), jnp.float32)
        tbl_1 = 0.05 * jax.random.normal(jax.random.fold_in(_tk, 500 + 1), (1000, 16), jnp.float32)
        tbl_2 = 0.05 * jax.random.normal(jax.random.fold_in(_tk, 500 + 2), (1250, 16), jnp.float32)
        tbl_3 = 0.05 * jax.random.normal(jax.random.fold_in(_tk, 500 + 3), (1000, 16), jnp.float32)
        tbl_4 = 0.05 * jax.random.normal(jax.random.fold_in(_tk, 500 + 4), (1250, 16), jnp.float32)
        tbl_5 = 0.05 * jax.random.normal(jax.random.fold_in(_tk, 500 + 5), (12500, 16), jnp.float32)
        tbl_6 = 0.05 * jax.random.normal(jax.random.fold_in(_tk, 500 + 6), (12500, 16), jnp.float32)
        tbl_7 = 0.05 * jax.random.normal(jax.random.fold_in(_tk, 500 + 7), (1250, 16), jnp.float32)
        tbl_8 = 0.05 * jax.random.normal(jax.random.fold_in(_tk, 500 + 8), (125000, 16), jnp.float32)
        tbl_9 = 0.05 * jax.random.normal(jax.random.fold_in(_tk, 500 + 9), (1000, 16), jnp.float32)
        tbl_10 = 0.05 * jax.random.normal(jax.random.fold_in(_tk, 500 + 10), (125000, 16), jnp.float32)
        tbl_11 = 0.05 * jax.random.normal(jax.random.fold_in(_tk, 500 + 11), (12500, 16), jnp.float32)
        tbl_12 = 0.05 * jax.random.normal(jax.random.fold_in(_tk, 500 + 12), (12500, 16), jnp.float32)
        tbl_13 = 0.05 * jax.random.normal(jax.random.fold_in(_tk, 500 + 13), (125000, 16), jnp.float32)
        tbl_14 = 0.05 * jax.random.normal(jax.random.fold_in(_tk, 500 + 14), (1250, 16), jnp.float32)
        tbl_15 = 0.05 * jax.random.normal(jax.random.fold_in(_tk, 500 + 15), (1000, 16), jnp.float32)
        tbl_16 = 0.05 * jax.random.normal(jax.random.fold_in(_tk, 500 + 16), (125000, 16), jnp.float32)
        tbl_17 = 0.05 * jax.random.normal(jax.random.fold_in(_tk, 500 + 17), (1250, 16), jnp.float32)
        tbl_18 = 0.05 * jax.random.normal(jax.random.fold_in(_tk, 500 + 18), (12500, 16), jnp.float32)
        tbl_19 = 0.05 * jax.random.normal(jax.random.fold_in(_tk, 500 + 19), (1250, 16), jnp.float32)
        tbl_20 = 0.05 * jax.random.normal(jax.random.fold_in(_tk, 500 + 20), (125000, 16), jnp.float32)
        tbl_21 = 0.05 * jax.random.normal(jax.random.fold_in(_tk, 500 + 21), (1000, 16), jnp.float32)
        tbl_22 = 0.05 * jax.random.normal(jax.random.fold_in(_tk, 500 + 22), (12500, 16), jnp.float32)
        tbl_23 = 0.05 * jax.random.normal(jax.random.fold_in(_tk, 500 + 23), (125000, 16), jnp.float32)
        tbl_24 = 0.05 * jax.random.normal(jax.random.fold_in(_tk, 500 + 24), (1000, 16), jnp.float32)
        tbl_25 = 0.05 * jax.random.normal(jax.random.fold_in(_tk, 500 + 25), (1000, 16), jnp.float32)
        tbl_26 = 0.05 * jax.random.normal(jax.random.fold_in(_tk, 500 + 26), (12500, 16), jnp.float32)
        tbl_27 = 0.05 * jax.random.normal(jax.random.fold_in(_tk, 500 + 27), (12500, 16), jnp.float32)
        tbl_28 = 0.05 * jax.random.normal(jax.random.fold_in(_tk, 500 + 28), (1250, 16), jnp.float32)
        tbl_29 = 0.05 * jax.random.normal(jax.random.fold_in(_tk, 500 + 29), (12500, 16), jnp.float32)
        tbl_30 = 0.05 * jax.random.normal(jax.random.fold_in(_tk, 500 + 30), (12500, 16), jnp.float32)
        tbl_31 = 0.05 * jax.random.normal(jax.random.fold_in(_tk, 500 + 31), (12500, 16), jnp.float32)
        tbl_32 = 0.05 * jax.random.normal(jax.random.fold_in(_tk, 500 + 32), (125000, 16), jnp.float32)
        tbl_33 = 0.05 * jax.random.normal(jax.random.fold_in(_tk, 500 + 33), (12500, 16), jnp.float32)
        tbl_34 = 0.05 * jax.random.normal(jax.random.fold_in(_tk, 500 + 34), (1250, 16), jnp.float32)
        tbl_35 = 0.05 * jax.random.normal(jax.random.fold_in(_tk, 500 + 35), (125000, 16), jnp.float32)
        tbl_36 = 0.05 * jax.random.normal(jax.random.fold_in(_tk, 500 + 36), (1000, 16), jnp.float32)
        tbl_37 = 0.05 * jax.random.normal(jax.random.fold_in(_tk, 500 + 37), (1250, 16), jnp.float32)
        tbl_38 = 0.05 * jax.random.normal(jax.random.fold_in(_tk, 500 + 38), (12500, 16), jnp.float32)
        _rk = jax.random.fold_in(_tk, 7)
        W_top1 = 0.05 * jax.random.normal(jax.random.fold_in(_tk, 801), (400, 512), jnp.float32)
        W_top2 = 0.0441942 * jax.random.normal(jax.random.fold_in(_tk, 802), (512, 256), jnp.float32)
        W_top3 = 0.0625 * jax.random.normal(jax.random.fold_in(_tk, 803), (256, 1), jnp.float32)
        b_top1 = jnp.zeros((512,), jnp.float32)
        b_top2 = jnp.zeros((256,), jnp.float32)
        return (dense_ctx, ids, tbl_0, tbl_1, tbl_2, tbl_3, tbl_4, tbl_5, tbl_6, tbl_7, tbl_8, tbl_9, tbl_10, tbl_11, tbl_12, tbl_13, tbl_14, tbl_15, tbl_16, tbl_17, tbl_18, tbl_19, tbl_20, tbl_21, tbl_22, tbl_23, tbl_24, tbl_25, tbl_26, tbl_27, tbl_28, tbl_29, tbl_30, tbl_31, tbl_32, tbl_33, tbl_34, tbl_35, tbl_36, tbl_37, tbl_38, W_top1, b_top1, W_top2, b_top2, W_top3)
    dense_ctx, ids, tbl_0, tbl_1, tbl_2, tbl_3, tbl_4, tbl_5, tbl_6, tbl_7, tbl_8, tbl_9, tbl_10, tbl_11, tbl_12, tbl_13, tbl_14, tbl_15, tbl_16, tbl_17, tbl_18, tbl_19, tbl_20, tbl_21, tbl_22, tbl_23, tbl_24, tbl_25, tbl_26, tbl_27, tbl_28, tbl_29, tbl_30, tbl_31, tbl_32, tbl_33, tbl_34, tbl_35, tbl_36, tbl_37, tbl_38, W_top1, b_top1, W_top2, b_top2, W_top3 = _rec_inputs()

    def _L0_rec_setup():
        import jax, jax.numpy as jnp
        import numpy as np
        B, F0, D = (256, 39, 16)
        CROSS = [128, 128, 128]
        key = jax.random.key(seed)
        k0, k1, k2, k3 = jax.random.split(key, 4)
        inputs = jax.random.normal(k0, (B, F0, D), dtype=jnp.float32)
        f0 = jax.random.normal(k1, (F0 * F0, CROSS[0]), dtype=jnp.float32) * 0.05
        f1 = jax.random.normal(k2, (CROSS[0] * F0, CROSS[1]), dtype=jnp.float32) * 0.05
        f2 = jax.random.normal(k3, (CROSS[1] * F0, CROSS[2]), dtype=jnp.float32) * 0.05
        return {'inputs': inputs, 'f0': f0, 'f1': f1, 'f2': f2}
    _L0_rec_all = _L0_rec_setup()
    _L0_rec_in = {k: v for k, v in _L0_rec_all.items() if k in ('f0', 'f1', 'f2')}
    del _L0_rec_all
    return {'dense_ctx': dense_ctx, 'ids': ids, 'tbl_0': tbl_0, 'tbl_1': tbl_1, 'tbl_2': tbl_2, 'tbl_3': tbl_3, 'tbl_4': tbl_4, 'tbl_5': tbl_5, 'tbl_6': tbl_6, 'tbl_7': tbl_7, 'tbl_8': tbl_8, 'tbl_9': tbl_9, 'tbl_10': tbl_10, 'tbl_11': tbl_11, 'tbl_12': tbl_12, 'tbl_13': tbl_13, 'tbl_14': tbl_14, 'tbl_15': tbl_15, 'tbl_16': tbl_16, 'tbl_17': tbl_17, 'tbl_18': tbl_18, 'tbl_19': tbl_19, 'tbl_20': tbl_20, 'tbl_21': tbl_21, 'tbl_22': tbl_22, 'tbl_23': tbl_23, 'tbl_24': tbl_24, 'tbl_25': tbl_25, 'tbl_26': tbl_26, 'tbl_27': tbl_27, 'tbl_28': tbl_28, 'tbl_29': tbl_29, 'tbl_30': tbl_30, 'tbl_31': tbl_31, 'tbl_32': tbl_32, 'tbl_33': tbl_33, 'tbl_34': tbl_34, 'tbl_35': tbl_35, 'tbl_36': tbl_36, 'tbl_37': tbl_37, 'tbl_38': tbl_38, 'W_top1': W_top1, 'b_top1': b_top1, 'W_top2': W_top2, 'b_top2': b_top2, 'W_top3': W_top3, 'L0_rec_f0': _L0_rec_in['f0'], 'L0_rec_f1': _L0_rec_in['f1'], 'L0_rec_f2': _L0_rec_in['f2']}

def reference(dense_ctx, ids, tbl_0, tbl_1, tbl_2, tbl_3, tbl_4, tbl_5, tbl_6, tbl_7, tbl_8, tbl_9, tbl_10, tbl_11, tbl_12, tbl_13, tbl_14, tbl_15, tbl_16, tbl_17, tbl_18, tbl_19, tbl_20, tbl_21, tbl_22, tbl_23, tbl_24, tbl_25, tbl_26, tbl_27, tbl_28, tbl_29, tbl_30, tbl_31, tbl_32, tbl_33, tbl_34, tbl_35, tbl_36, tbl_37, tbl_38, W_top1, b_top1, W_top2, b_top2, W_top3, L0_rec_f0, L0_rec_f1, L0_rec_f2):
    import jax
    import jax.numpy as jnp

    def _L0_rec_ref(inputs, f0, f1, f2):
        import jax, jax.numpy as jnp
        import numpy as np
        B, F0, D = (256, 39, 16)
        CROSS = [128, 128, 128]
        filters = [f0, f1, f2]
        x0 = inputs
        xk = inputs
        outs = []
        for W in filters:
            b, f, d = x0.shape
            g = xk.shape[1]
            z = jnp.einsum('bfd,bgd->bfgd', x0, xk).reshape(b, f * g, d)
            cur = jnp.einsum('bpd,pm->bmd', z, W)
            outs.append(cur)
            xk = cur
        result = jnp.concatenate(outs, axis=1)
        return jnp.sum(result, axis=-1)
    e = jnp.stack([tbl_0[ids[:, 0]], tbl_1[ids[:, 1]], tbl_2[ids[:, 2]], tbl_3[ids[:, 3]], tbl_4[ids[:, 4]], tbl_5[ids[:, 5]], tbl_6[ids[:, 6]], tbl_7[ids[:, 7]], tbl_8[ids[:, 8]], tbl_9[ids[:, 9]], tbl_10[ids[:, 10]], tbl_11[ids[:, 11]], tbl_12[ids[:, 12]], tbl_13[ids[:, 13]], tbl_14[ids[:, 14]], tbl_15[ids[:, 15]], tbl_16[ids[:, 16]], tbl_17[ids[:, 17]], tbl_18[ids[:, 18]], tbl_19[ids[:, 19]], tbl_20[ids[:, 20]], tbl_21[ids[:, 21]], tbl_22[ids[:, 22]], tbl_23[ids[:, 23]], tbl_24[ids[:, 24]], tbl_25[ids[:, 25]], tbl_26[ids[:, 26]], tbl_27[ids[:, 27]], tbl_28[ids[:, 28]], tbl_29[ids[:, 29]], tbl_30[ids[:, 30]], tbl_31[ids[:, 31]], tbl_32[ids[:, 32]], tbl_33[ids[:, 33]], tbl_34[ids[:, 34]], tbl_35[ids[:, 35]], tbl_36[ids[:, 36]], tbl_37[ids[:, 37]], tbl_38[ids[:, 38]]], axis=1)
    z = _L0_rec_ref(e, L0_rec_f0, L0_rec_f1, L0_rec_f2)
    z = z.reshape(z.shape[0], -1)
    h = jnp.concatenate([z, dense_ctx], axis=1)
    h = jnp.maximum(h @ W_top1 + b_top1, 0.0)
    h = jnp.maximum(h @ W_top2 + b_top2, 0.0)
    y = h @ W_top3
    return y

_drawn_inputs = setup_inputs


def setup_inputs(seed=0):
    import zlib

    import numpy as np

    out = dict(_drawn_inputs(seed))
    spreads = {'b_top1': (0.0, 0.594), 'b_top2': (0.0, 0.277)}
    factors = {'tbl_0': 4.608,
     'tbl_1': 5.225,
     'tbl_2': 4.448,
     'tbl_3': 4.911,
     'tbl_4': 5.058,
     'tbl_5': 4.803,
     'tbl_6': 4.384,
     'tbl_7': 4.775,
     'tbl_8': 5.001,
     'tbl_9': 4.737,
     'tbl_10': 5.205,
     'tbl_11': 4.699,
     'tbl_12': 4.453,
     'tbl_13': 4.349,
     'tbl_14': 4.772,
     'tbl_15': 4.71,
     'tbl_16': 5.316,
     'tbl_17': 4.901,
     'tbl_18': 4.995,
     'tbl_19': 4.849,
     'tbl_20': 4.779,
     'tbl_21': 4.708,
     'tbl_22': 4.577,
     'tbl_23': 4.956,
     'tbl_24': 4.878,
     'tbl_25': 4.387,
     'tbl_26': 5.19,
     'tbl_27': 5.029,
     'tbl_28': 4.76,
     'tbl_29': 4.997,
     'tbl_30': 4.838,
     'tbl_31': 4.472,
     'tbl_32': 5.077,
     'tbl_33': 5.096,
     'tbl_34': 4.54,
     'tbl_35': 4.79,
     'tbl_36': 4.434,
     'tbl_37': 5.333,
     'tbl_38': 4.88,
     'L0_rec_f1': 5.264,
     'L0_rec_f2': 8.0}
    for name, (base, spread) in spreads.items():
        noise = np.random.default_rng([zlib.crc32(name.encode()), seed]).standard_normal(out[name].shape)
        drawn = base * np.exp(spread * noise) if base else spread * noise
        out[name] = jnp.asarray(drawn.astype(out[name].dtype))
    for name, factor in factors.items():
        out[name] = (out[name] * factor).astype(out[name].dtype)
    return out
```

```python
import concourse.bass as bass
from concourse import mybir
from contextlib import ExitStack

B, F0, D, M = 512, 39, 16, 128
CH = 128
NCH = B // CH
TB = 128 // D
TPC = CH // TB
POS = CH * D
FP = F0 + 1
NS = (F0 + 1) // 2
SHIFTS = list(range(1, NS)) + [0]
SPT = 3
PAIR_TILES = [SHIFTS[i:i + SPT] for i in range(0, NS, SPT)]
NK = len(PAIR_TILES)
NG = POS // 512

GROUPS = [list(range(f, min(f + 4, F0))) for f in range(0, F0, 4)]
NQ = len(GROUPS)
RING = 5
ACT_Q = [0, 2, 3, 5, 6, 8]
DVE_Q = [q for q in range(NQ) if q not in ACT_Q]
NA = len(ACT_Q)
PRODS = 3
STEPS = NQ
GRAM_AFTER = 6


def step_of(q):
    return max(q - 1, 0)


USES_X0T, USES_X0P, USES_L1 = 4, 2, NG
USES_PREP = USES_X0T + USES_X0P + USES_L1
USES_TAIL = 4
USES = USES_PREP + USES_TAIL
assert USES_PREP % 2 == 0 and USES % 2 == 0


def build(nc, t):
    fp32, i32, u32 = mybir.dt.float32, mybir.dt.int32, mybir.dt.uint32
    ALU, ACT, AX = mybir.AluOpType, mybir.ActivationFunctionType, mybir.AxisListType
    ctx = ExitStack()
    with ctx:
        def sb(name, shape, dt=fp32):
            return ctx.enter_context(nc.sbuf_tensor(name, shape, dt))

        def sem(name):
            return ctx.enter_context(nc.semaphore(name))

        ids_now = sb("ids_now", [CH, F0], i32)
        rows = sb("rows", [CH, SPT * F0, D])
        x0rep = sb("x0rep", [SPT * F0, CH, D])
        pairs = sb("pairs", [SPT * F0, NK, POS])
        x0pos = sb("x0pos", [128, TPC, FP])
        x0diag = sb("x0diag", [128, TPC, TB, FP])
        x1T = sb("x1T", [M, POS])
        w1 = sb("w1", [SPT * F0, NK, M])
        w2 = sb("w2", [M, F0, M])
        w3 = sb("w3", [M, F0, M])
        prod = sb("prod", [128, PRODS, 512])
        acc = sb("acc", [128, 512])
        half = sb("half", [128, 256])
        x2 = sb("x2", [128, TPC, M])
        gram = sb("gram", [M, FP, CH])
        w1t = gram[0:SPT * F0, 0:NK, :]
        sum1 = sb("sum1", [M, CH])
        s3 = sb("s3", [M, CH])
        denseT = sb("denseT", [D, B])
        wt1 = sb("wt1", [128, 3, 512])
        wt1d = sb("wt1d", [D, 512])
        bt1 = sb("bt1", [128, 4])
        wt2 = sb("wt2", [128, 4, 256])
        bt2 = sb("bt2", [128, 2])
        wt3 = sb("wt3", [128, 2])
        h1 = sb("h1", [128, 4, CH])
        h2 = sb("h2", [128, 2, CH])
        y = sb("y", [1, B])
        ident = sb("ident", [128, 128])
        rowmask = sb("rowmask", [128, TB])
        warm = sb("warm", [128, 1])

        ybank = [ctx.enter_context(nc.psum_tensor(f"ybank{i}", [128, 512], fp32)) for i in range(RING)]
        aux = [ctx.enter_context(nc.psum_tensor(f"aux{i}", [128, 512], fp32)) for i in range(2)]
        gbank = ctx.enter_context(nc.psum_tensor("gbank", [128, 512], fp32))

        w1_in, w2_in, w3_in, top_in = sem("w1_in"), sem("w2_in"), sem("w3_in"), sem("top_in")
        ids_in = sem("ids_in")
        rows_in = sem("rows_in")
        rows_tripled = sem("rows_tripled")
        rows_used = sem("rows_used")
        const_step = sem("const_step")
        w1_ready = sem("w1_ready")
        x0rep_ready = sem("x0rep_ready")
        shifted_in = [sem(f"shifted_in{k}") for k in range(NK)]
        pairs_ready = sem("pairs_ready")
        x0pos_ready = sem("x0pos_ready")
        diag_ready = sem("diag_ready")
        x1_ready = sem("x1_ready")
        sum1_ready = sem("sum1_ready")
        y_ready = sem("y_ready")
        prod_ready = sem("prod_ready")
        acc_step = sem("acc_step")
        x2_ready = sem("x2_ready")
        gram_ready = sem("gram_ready")
        gram_drained = sem("gram_drained")
        aux_full, aux_drained = sem("aux_full"), sem("aux_drained")
        out_done = sem("out_done")
        CONSTS = 7

        block = ctx.enter_context(nc.Block())

        @block.sync
        def _(sp):
            sp.dma_start(ids_now[:], t["ids"][0:CH, :]).then_inc(ids_in, 16)
            sp.dma_start(w1[:, 0:NK - 1, :], t["w1a"][0:(NK - 1) * SPT * F0, :]
                         .rearrange("(k p) m -> p k m", p=SPT * F0)).then_inc(w1_in, 16)
            sp.dma_start(w1[0:2 * F0, NK - 1, :], t["w1a"][(NK - 1) * SPT * F0:, :]).then_inc(w1_in, 16)
            sp.dma_start(w1t[:, 0:NK - 1, :], t["w1b"][0:(NK - 1) * SPT * F0, :]
                         .rearrange("(k p) m -> p k m", p=SPT * F0)).then_inc(w1_in, 16)
            sp.dma_start(w1t[0:F0, NK - 1, :], t["w1b"][(NK - 1) * SPT * F0:, :]).then_inc(w1_in, 16)

            def shift(c):
                sp.wait_ge(x0rep_ready, c + 1)
                if not (isinstance(c, int) and c == 0):
                    sp.wait_ge(aux_full, c * USES + (USES_PREP - USES))
                for k, shifts in enumerate(PAIR_TILES):
                    for j, s in enumerate(shifts):
                        sp.dma_start(pairs[j * F0:(j + 1) * F0, k, :],
                                     x0rep[s:s + F0, :, :].rearrange("p b d -> p (b d)")).then_inc(shifted_in[k], 16)

            def next_ids(c):
                sp.wait_ge(rows_in, 16 * F0 * c)
                sp.dma_start(ids_now[:], t["ids"][bass.ds(c * CH, CH), :]).then_inc(ids_in, 16)

            next_ids(1)
            shift(0)
            with sp.Fori(1, NCH - 1) as c:
                next_ids(c + 1)
                shift(c)
            shift(NCH - 1)
            sp.wait_ge(aux_drained, USES_PREP * 1 + USES * (NCH - 1) + USES_TAIL)
            sp.dma_start(t["out"].rearrange("b o -> o b"), y[:]).then_inc(out_done, 16)
            sp.wait_ge(out_done, 16)

        @block.gpsimd
        def _(pool):
            nc.gpsimd.memset(ident[:], 0.0).then_inc(const_step, 1)
            nc.gpsimd.memset(rowmask[:], 1.0).then_inc(const_step, 1)
            nc.gpsimd.memset(x0pos[:, :, F0:FP], 1.0).then_inc(const_step, 1)
            nc.gpsimd.memset(warm[:], 0.0).then_inc(const_step, 1)
            pool.wait_ge(const_step, 4)
            nc.gpsimd.affine_select(out=ident[:], in_=ident[:], compare_op=ALU.not_equal, fill=1.0, base=0,
                                    pattern=[[-1, 128]], channel_multiplier=1).then_inc(const_step, 1)
            nc.gpsimd.affine_select(out=rowmask[:], in_=rowmask[:], compare_op=ALU.is_ge, fill=0.0, base=0,
                                    pattern=[[-D, TB]], channel_multiplier=1).then_inc(const_step, 1)
            pool.wait_ge(const_step, 6)
            nc.gpsimd.affine_select(out=rowmask[:], in_=rowmask[:], compare_op=ALU.is_ge, fill=0.0, base=D - 1,
                                    pattern=[[D, TB]], channel_multiplier=-1).then_inc(const_step, 1)
            pool.wait_ge(const_step, CONSTS)

            def wait_gather(c):
                pool.wait_ge(ids_in, 16 * (c + 1))
                pool.wait_ge(rows_used, c)

            def gather():
                for f in range(F0):
                    nc.gpsimd.indirect_dma_start(
                        rows[:, f, :], None, t["tables"][f],
                        bass.IndirectOffsetOnAxis(ap=ids_now[:, f:f + 1].bitcast(u32), axis=0)).then_inc(rows_in, 16)

            def multiply_pairs(c):
                for k, shifts in enumerate(PAIR_TILES):
                    n = F0 * len(shifts)
                    pool.wait_ge(shifted_in[k], (c + 1) * (16 * len(shifts)))
                    nc.gpsimd.tensor_tensor(pairs[0:n, k, :], pairs[0:n, k, :],
                                            x0rep[0:n, :, :].rearrange("p b d -> p (b d)"),
                                            ALU.mult).then_inc(pairs_ready, 1)

            def spread_x0():
                for tt in range(TPC):
                    last = nc.gpsimd.tensor_tensor(
                        x0diag[:, tt, :, :], x0pos[:, tt, :].unsqueeze(1).broadcast_to([128, TB, FP]),
                        rowmask[:].unsqueeze(2).broadcast_to([128, TB, FP]), ALU.mult)
                last.then_inc(diag_ready, 1)

            wait_gather(0)
            gather()
            with pool.Fori(0, NCH - 1) as c:
                multiply_pairs(c)
                wait_gather(c + 1)
                pool.wait_ge(gram_ready, c * TPC)
                pool.wait_ge(x0pos_ready, c + 1)
                spread_x0()
                gather()
            multiply_pairs(NCH - 1)
            pool.wait_ge(gram_ready, (NCH - 1) * TPC)
            pool.wait_ge(x0pos_ready, NCH)
            spread_x0()

        @block.tensor
        def _(pe):
            def take_aux(n, u):
                if not (isinstance(n, int) and n < 2):
                    pe.wait_ge(aux_drained, n - 1)
                return aux[u % 2]

            def x0_transposed(c, n):
                pe.wait_ge(rows_tripled, 2 * (c + 1))
                for u in range(USES_X0T):
                    bank = take_aux(n + u, u)
                    for j in range(4):
                        d = 4 * u + j
                        last = nc.tensor.transpose(
                            bank[0:SPT * F0, j * CH:(j + 1) * CH],
                            rows[:, :, d], ident[:])
                    if u == USES_X0T - 1:
                        last.then_inc(rows_used, 1)
                        pe.wait_ge(rows_used, c + 1)
                        pe.sem_inc(aux_full, 1)
                    else:
                        last.then_inc(aux_full, 1)

            def wait_positions(c):
                pe.wait_ge(x0rep_ready, c + 1)

            def x0_positions():
                for u in range(USES_X0P):
                    bank = aux[u % 2]
                    for j in range(TPC // 2):
                        tt = u * (TPC // 2) + j
                        last = nc.tensor.transpose(
                            bank[:, j * FP:j * FP + F0],
                            x0rep[0:F0, tt * TB:(tt + 1) * TB, :].rearrange("p b d -> p (b d)"), ident[0:F0, 0:F0])
                    last.then_inc(aux_full, 1)

            def layer1(c, n, g):
                bank = take_aux(n + g, g)
                for k, shifts in enumerate(PAIR_TILES):
                    r = F0 * len(shifts)
                    if g == 0:
                        pe.wait_ge(pairs_ready, c * NK + (k + 1))
                    last = nc.tensor.matmul(bank[:], w1[0:r, k, :], pairs[0:r, k, 512 * g:512 * (g + 1)],
                                            start=(k == 0), stop=(k == NK - 1))
                last.then_inc(aux_full, 1)

            def gram_product(c, tt):
                if tt == 0:
                    pe.wait_ge(diag_ready, c + 1)
                pe.wait_ge(x2_ready, c * TPC + (tt + 1))
                pe.wait_ge(gram_drained, c * TPC + tt)
                nc.tensor.matmul(gbank[:, 0:TB * FP], x2[:, tt, :],
                                 x0diag[:, tt, :, :].rearrange("p r f -> p (r f)"),
                                 start=True, stop=True).then_inc(gram_ready, 1)

            def tile(c, tt):
                for q, feats in enumerate(GROUPS):
                    before, back = (q - RING, 1) if q >= RING else (q - RING + NQ, 0)
                    if before in ACT_Q:
                        pe.wait_ge(prod_ready, c * (TPC * NA) + ((tt + back) * NA + ACT_Q.index(before) + 1))
                    else:
                        pe.wait_ge(acc_step, c * (TPC * STEPS) + ((tt + back) * STEPS + step_of(before) + 1))
                    n = len(feats) * M
                    nc.tensor.matmul(ybank[q % RING][:, 0:n], x1T[:, tt * 128:(tt + 1) * 128],
                                     w2[:, feats[0]:feats[-1] + 1, :].rearrange("p f m -> p (f m)"),
                                     start=True, stop=True).then_inc(y_ready, 1)
                    if q == GRAM_AFTER and tt > 0:
                        gram_product(c, tt - 1)

            def layer3_and_mlp(c, n):
                pe.wait_ge(gram_drained, (c + 1) * TPC)
                bank = take_aux(n, 0)
                for f in range(F0):
                    last = nc.tensor.matmul(bank[:, 0:CH], w3[:, f, :], gram[:, f, :],
                                            start=(f == 0), stop=(f == F0 - 1))
                last.then_inc(aux_full, 1)
                bank = take_aux(n + 1, 1)
                pe.wait_ge(sum1_ready, c + 1)
                pe.wait_ge(aux_drained, n + 1)
                for i in range(4):
                    cols = slice(i * 128, (i + 1) * 128)
                    nc.tensor.matmul(bank[:, cols], wt1[:, 0, cols], sum1[:], start=True, stop=False)
                    nc.tensor.matmul(bank[:, cols], wt1[:, 1, cols], gram[:, F0, :], start=False, stop=False)
                    nc.tensor.matmul(bank[:, cols], wt1[:, 2, cols], s3[:], start=False, stop=False)
                    last = nc.tensor.matmul(bank[:, cols], wt1d[:, cols], denseT[:, bass.ds(c * CH, CH)],
                                            start=False, stop=True)
                last.then_inc(aux_full, 1)
                bank = take_aux(n + 2, 2)
                pe.wait_ge(aux_drained, n + 2)
                for i in range(2):
                    for k in range(4):
                        last = nc.tensor.matmul(bank[:, i * CH:(i + 1) * CH], wt2[:, k, i * 128:(i + 1) * 128],
                                                h1[:, k, :], start=(k == 0), stop=(k == 3))
                last.then_inc(aux_full, 1)
                bank = take_aux(n + 3, 3)
                pe.wait_ge(aux_drained, n + 3)
                for k in range(2):
                    last = nc.tensor.matmul(bank[0:1, 0:CH], wt3[:, k:k + 1], h2[:, k, :],
                                            start=(k == 0), stop=(k == 1))
                last.then_inc(aux_full, 1)

            pe.wait_ge(const_step, CONSTS)
            x0_transposed(0, 0)
            wait_positions(0)
            x0_positions()
            pe.wait_ge(w1_ready, 2)
            for g in range(NG):
                layer1(0, USES_X0T + USES_X0P, g)
            pe.wait_ge(w2_in, 16)
            pe.wait_ge(w3_in, 16)
            pe.wait_ge(top_in, 16 * 7)

            def chunk(c, last):
                n = USES_PREP + c * USES
                pe.wait_ge(x1_ready, c + 1)
                for tt in range(TPC // 2):
                    tile(c, tt)
                if not last:
                    x0_transposed(c + 1, n)
                for tt in range(TPC // 2, TPC):
                    if tt == TPC - 1 and not last:
                        wait_positions(c + 1)
                    tile(c, tt)
                if last:
                    gram_product(c, TPC - 1)
                    layer3_and_mlp(c, n)
                else:
                    x0_positions()
                    for g in range(NG):
                        layer1(c + 1, n + USES_X0T + USES_X0P, g)
                        if g == 0:
                            gram_product(c, TPC - 1)
                    layer3_and_mlp(c, n + USES_PREP)

            with pe.Fori(0, NCH - 1) as c:
                chunk(c, False)
            chunk(NCH - 1, True)

        @block.scalar
        def _(act):
            act.dma_start(w2[:], t["f1"].rearrange("(f g) m -> g f m", g=M)).then_inc(w2_in, 16)
            act.dma_start(w3[:], t["f2"].rearrange("(f g) m -> g f m", g=M)).then_inc(w3_in, 16)
            act.dma_start(wt1[:], t["wt1"][0:384, :].rearrange("(k p) n -> p k n", p=128)).then_inc(top_in, 16)
            act.dma_start(wt1d[:], t["wt1"][384:400, :]).then_inc(top_in, 16)
            act.dma_start(wt2[:], t["wt2"].rearrange("(k p) n -> p k n", p=128)).then_inc(top_in, 16)
            act.dma_start(bt1[:], t["bt1"]).then_inc(top_in, 16)
            act.dma_start(bt2[:], t["bt2"]).then_inc(top_in, 16)
            act.dma_start(wt3[:], t["wt3"]).then_inc(top_in, 16)
            act.dma_start(denseT[:], t["denseT"]).then_inc(top_in, 16)
            act.wait_ge(const_step, CONSTS)
            nc.scalar.activation(warm[:], ident[:, 0:1], ACT.Copy)
            act.sem_inc(prod_ready, NA)

            def drained(n, ins):
                ins.then_inc(aux_drained, 1)

            def x0_transposed(c, n):
                act.wait_ge(rows_in, 16 * F0 * (c + 1))
                for j in range(1, SPT):
                    nc.scalar.copy(rows[:, j * F0:(j + 1) * F0, :], rows[:, 0:F0, :]).then_inc(rows_tripled, 1)
                act.wait_ge(pairs_ready, c * NK)
                for u in range(USES_X0T):
                    act.wait_ge(aux_full, n + (u + 1))
                    last = nc.scalar.copy(
                        x0rep[:, :, 4 * u:4 * (u + 1)].rearrange("p b d -> p d b"),
                        aux[u % 2][0:SPT * F0, :].rearrange("p (d b) -> p d b", d=4))
                    last.then_inc(aux_drained, 1)
                act.wait_ge(aux_drained, n + USES_X0T)
                act.sem_inc(x0rep_ready, 1)

            def x0_positions(c, n):
                act.wait_ge(x2_ready, c * TPC)
                act.wait_ge(diag_ready, c)
                for u in range(USES_X0P):
                    act.wait_ge(aux_full, n + (u + 1))
                    nc.scalar.copy(x0pos[:, u * (TPC // 2):(u + 1) * (TPC // 2), 0:F0],
                                   aux[u % 2][:, 0:(TPC // 2) * FP].rearrange("p (t f) -> p t f", f=FP)[:, :, 0:F0]
                                   ).then_inc(aux_drained, 1)
                act.wait_ge(aux_drained, n + USES_X0P)
                act.sem_inc(x0pos_ready, 1)

            def layer1(c, n, g):
                if g == 0:
                    act.wait_ge(sum1_ready, c)
                act.wait_ge(aux_full, n + (g + 1))
                nc.scalar.copy(x1T[:, 512 * g:512 * (g + 1)], aux[g % 2][:]).then_inc(aux_drained, 1)
                if g == NG - 1:
                    act.wait_ge(aux_drained, n + NG)
                    act.sem_inc(x1_ready, 1)

            def gram_out(c, tt):
                act.wait_ge(gram_ready, c * TPC + (tt + 1))
                nc.scalar.copy(gram[:, :, bass.ds(tt * TB, TB)].rearrange("p f r -> p r f"),
                               gbank[:, 0:TB * FP].rearrange("p (r f) -> p r f", f=FP)).then_inc(gram_drained, 1)

            def tile(c, tt, with_gram):
                for i, q in enumerate(ACT_Q):
                    ahead = STEPS if i >= PRODS else 0
                    act.wait_ge(acc_step, c * (TPC * STEPS) + tt * STEPS + (ahead + step_of(ACT_Q[(i - PRODS) % NA]) + 1))
                    act.wait_ge(y_ready, c * (TPC * NQ) + tt * NQ + (q + 1))
                    for j, f in enumerate(GROUPS[q]):
                        last = nc.scalar.activation(prod[:, i % PRODS, j * M:(j + 1) * M],
                                                    ybank[q % RING][:, j * M:(j + 1) * M], ACT.Copy,
                                                    scale=x0pos[:, bass.ds(tt, 1), f:f + 1].rearrange("p t f -> p (t f)"))
                    last.then_inc(prod_ready, 1)
                    if q == GRAM_AFTER and with_gram:
                        gram_out(c, tt - 1)

            def tail(c, n):
                act.wait_ge(aux_full, n + 1)
                nc.scalar.copy(s3[:], aux[0][:, 0:CH]).then_inc(aux_drained, 1)
                act.wait_ge(aux_full, n + 2)
                for i in range(4):
                    last = nc.scalar.activation(h1[:, i, :], aux[1][:, i * CH:(i + 1) * CH], ACT.Relu,
                                                bias=bt1[:, i:i + 1])
                last.then_inc(aux_drained, 1)
                act.wait_ge(aux_full, n + 3)
                for i in range(2):
                    last = nc.scalar.activation(h2[:, i, :], aux[0][:, i * CH:(i + 1) * CH], ACT.Relu,
                                                bias=bt2[:, i:i + 1])
                last.then_inc(aux_drained, 1)
                act.wait_ge(aux_full, n + 4)
                nc.scalar.copy(y[:, bass.ds(c * CH, CH)], aux[1][0:1, 0:CH]).then_inc(aux_drained, 1)

            x0_transposed(0, 0)
            x0_positions(0, USES_X0T)
            for g in range(NG):
                layer1(0, USES_X0T + USES_X0P, g)
            act.wait_ge(top_in, 16 * 7)

            def chunk(c, last):
                n = USES_PREP + c * USES
                act.wait_ge(x0pos_ready, c + 1)
                tile(c, 0, False)
                with act.Fori(1, TPC // 2) as tt:
                    tile(c, tt, True)
                if not last:
                    x0_transposed(c + 1, n)
                with act.Fori(TPC // 2, TPC) as tt:
                    tile(c, tt, True)
                if last:
                    gram_out(c, TPC - 1)
                    tail(c, n)
                else:
                    x0_positions(c + 1, n + USES_X0T)
                    for g in range(NG):
                        layer1(c + 1, n + USES_X0T + USES_X0P, g)
                        if g == 0:
                            gram_out(c, TPC - 1)
                    tail(c, n + USES_PREP)

            with act.Fori(0, NCH - 1) as c:
                chunk(c, False)
            chunk(NCH - 1, True)

        @block.vector
        def _(dve):
            dve.sem_inc(acc_step, STEPS)
            dve.wait_ge(w1_in, 16 * 4)
            nc.vector.tensor_tensor(w1[:, 0:NK - 1, :], w1[:, 0:NK - 1, :], w1t[:, 0:NK - 1, :],
                                    ALU.add).then_inc(w1_ready, 1)
            nc.vector.tensor_tensor(w1[0:F0, NK - 1, :], w1[0:F0, NK - 1, :], w1t[0:F0, NK - 1, :],
                                    ALU.add).then_inc(w1_ready, 1)

            with dve.Fori(0, NCH) as c:
                dve.wait_ge(x1_ready, c + 1)
                dve.wait_ge(aux_full, c * USES + USES_PREP)
                dve.wait_ge(x0pos_ready, c + 1)
                dve.wait_ge(gram_ready, c * TPC)
                nc.vector.tensor_reduce(sum1[:], x1T[:].rearrange("p (b d) -> p b d", d=D), AX.X,
                                        ALU.add).then_inc(sum1_ready, 1)
                with dve.Fori(0, TPC) as tt:
                    done = c * (TPC * STEPS) + (tt + 1) * STEPS

                    def scaled_group(q, addend):
                        dve.wait_ge(y_ready, c * (TPC * NQ) + tt * NQ + (q + 1))
                        for j, f in enumerate(GROUPS[q]):
                            cols = slice(j * M, (j + 1) * M)
                            last = nc.vector.scalar_tensor_tensor(
                                out=acc[:, cols], in0=ybank[q % RING][:, cols],
                                scalar=x0pos[:, bass.ds(tt, 1), f:f + 1].rearrange("p t f -> p (t f)"),
                                in1=addend[:, cols], op0=ALU.mult, op1=ALU.add)
                        last.then_inc(acc_step, 1)

                    for q in range(1, NQ):
                        dve.wait_ge(acc_step, done + step_of(q))
                        if q == 1:
                            dve.wait_ge(prod_ready, c * (TPC * NA) + (tt + 1) * NA + 1)
                            scaled_group(1, prod[:, 0, :])
                        elif q in DVE_Q:
                            scaled_group(q, acc)
                        else:
                            i = ACT_Q.index(q)
                            dve.wait_ge(prod_ready, c * (TPC * NA) + (tt + 1) * NA + (i + 1))
                            nc.vector.tensor_tensor(acc[:], acc[:], prod[:, i % PRODS, :], ALU.add).then_inc(acc_step, 1)
                    dve.wait_ge(acc_step, done + (STEPS - 1))
                    nc.vector.tensor_tensor(half[:], acc[:, 0:256], acc[:, 256:512], ALU.add).then_inc(acc_step, 1)
                    dve.wait_ge(acc_step, done + STEPS)
                    nc.vector.tensor_tensor(x2[:, bass.ds(tt, 1), :].rearrange("p t m -> p (t m)"), half[:, 0:128],
                                            half[:, 128:256], ALU.add).then_inc(x2_ready, 1)


def pair_rows():
    fg = [(f, (f + s) % F0) for s in SHIFTS for f in range(F0)]
    return [f * F0 + g for f, g in fg], [g * F0 + f for f, g in fg[:(NS - 1) * F0]]


def kernel(**inputs):
    import numpy as np
    import concourse.bacc as bacc
    from concourse.bass_utils import run_bass_kernel_spmd

    nc = bacc.Bacc("TRN2", target_bir_lowering=False, num_devices=1)
    arrays = {}

    def dram(name, a):
        a = np.ascontiguousarray(a)
        name = f"in_{name}"
        arrays[name] = a
        return nc.dram_tensor(name, a.shape, mybir.dt.from_np(a.dtype), kind="ExternalInput").ap()

    first, second = pair_rows()
    f0 = np.asarray(inputs["L0_rec_f0"])
    t = {
        "ids": dram("ids", inputs["ids"]),
        "tables": [dram(f"table{f}", inputs[f"tbl_{f}"]) for f in range(F0)],
        "w1a": dram("w1a", f0[first]),
        "w1b": dram("w1b", f0[second]),
        "f1": dram("f1", inputs["L0_rec_f1"]),
        "f2": dram("f2", inputs["L0_rec_f2"]),
        "denseT": dram("denseT", np.asarray(inputs["dense_ctx"]).T),
        "wt1": dram("wt1", inputs["W_top1"]),
        "wt2": dram("wt2", inputs["W_top2"]),
        "bt1": dram("bt1", np.asarray(inputs["b_top1"]).reshape(4, 128).T),
        "bt2": dram("bt2", np.asarray(inputs["b_top2"]).reshape(2, 128).T),
        "wt3": dram("wt3", np.asarray(inputs["W_top3"]).reshape(2, 128).T),
        "out": nc.dram_tensor("out", (B, 1), mybir.dt.float32, kind="ExternalOutput").ap(),
    }
    build(nc, t)
    r = run_bass_kernel_spmd(nc, [arrays], core_ids=[0])
    return r.results[0]["out"]
```

```python
import concourse.bass as bass
from concourse import mybir
from contextlib import ExitStack

B, F0, D, M = 512, 39, 16, 128
CH = 128
NCH = B // CH
TB = 128 // D
TPC = CH // TB
POS = CH * D
FP = F0 + 1
NS = (F0 + 1) // 2
SHIFTS = list(range(1, NS)) + [0]
SPT = 3
PAIR_TILES = [SHIFTS[i:i + SPT] for i in range(0, NS, SPT)]
NK = len(PAIR_TILES)
NG = POS // 512
GT = TPC // NG
GB = CH // NG

GROUPS = [list(range(f, min(f + 4, F0))) for f in range(0, F0, 4)]
NQ = len(GROUPS)
RING = 5
ACT_Q = [0, 2, 3, 5, 6, 8]
DVE_Q = [q for q in range(NQ) if q not in ACT_Q]
NA = len(ACT_Q)
PRODS = 3
GRAM_AFTER = 8
STEPS = [("scale", [1, 0]), ("scale", [4]), ("add", [2, 3]), ("add", [5]), ("scale", [7]),
         ("add", [6]), ("scale", [9]), ("add", [8])]
NSTEPS = len(STEPS)


def step_of(q):
    return next(i for i, (_, used) in enumerate(STEPS) if q in used)


def step_before(i):
    earlier = [n for n in range(i) if STEPS[n][0] == STEPS[i][0]]
    return earlier[-1] + 1 if earlier else 0


EVENTS = [(0, "layer3", 0), (0, "x0P", NG - 1), (0, "x0T", 0), (1, "mlp1", 0), (2, "mlp2", 0), (3, "mlp3", 0),
          (3, "layer1", 0), (4, "x0P", 0), (7, "layer1", 1), (8, "x0P", 1), (11, "layer1", 2), (12, "x0P", 2),
          (15, "layer1", 3)]
TAIL = ["layer3", "mlp1", "mlp2", "mlp3"]
X0T_USES = D // 4
PROLOGUE = [("x0T", 0)] + [("x0P", g) for g in range(NG - 1)] + [("layer1", g) for g in range(NG)]


def uses_of(what):
    return X0T_USES if what == "x0T" else 1


def events(first, last):
    out, n = [], 0
    for tile, what, g in EVENTS:
        if (first and what in TAIL) or (last and what not in TAIL and (what, g) != ("x0P", NG - 1)):
            continue
        out.append((tile, what, g, n))
        n += uses_of(what)
    return out, n


USES = events(False, False)[1]
USES0 = sum(uses_of(what) for what, _ in PROLOGUE)
BASE = USES0 + events(True, False)[1] - USES
assert USES % 2 == 0 and BASE > 0


def bank_of(use):
    return use[0] % 2


def filled(use):
    return use[1] * USES + (use[0] + 1)


def free_before(use):
    return use[1] * (USES // 2) + use[0] // 2


def taken_out(use):
    return use[1] * (USES // 2) + (use[0] // 2 + 1)


def zero(c):
    return isinstance(c, int) and c == 0


def build(nc, t):
    fp32, fp32r, i32, u32 = mybir.dt.float32, mybir.dt.float32r, mybir.dt.int32, mybir.dt.uint32
    ALU, ACT, AX = mybir.AluOpType, mybir.ActivationFunctionType, mybir.AxisListType
    ctx = ExitStack()
    with ctx:
        def sb(name, shape, dt=fp32):
            return ctx.enter_context(nc.sbuf_tensor(name, shape, dt))

        def sem(name):
            return ctx.enter_context(nc.semaphore(name))

        row_ids = sb("row_ids", [CH, 2, F0], i32)
        rows1 = sb("rows1", [CH, F0, D])
        rows = sb("rows", [CH, SPT * F0, D])
        x0rep = sb("x0rep", [SPT * F0, CH, D])
        pairs = sb("pairs", [SPT * F0, 2, NK, 512])
        x0pos = sb("x0pos", [128, TPC, FP])
        x0diag = sb("x0diag", [128, 2, GT, TB, FP])
        x1h = sb("x1h", [M, POS], fp32r)
        x1l = sb("x1l", [M, POS], fp32r)
        w1 = sb("w1", [SPT * F0, NK, M])
        w2h = sb("w2h", [M, F0, M], fp32r)
        w2l = sb("w2l", [M, F0, M], fp32r)
        w3 = sb("w3", [M, F0, M])
        prod = sb("prod", [128, PRODS, 512])
        scaled = sb("scaled", [128, 2, 512])
        added = sb("added", [128, 2, 512])
        both = sb("both", [128, 512])
        x2 = sb("x2", [128, GT, M])
        gram = sb("gram", [M, FP, CH])
        w2raw = gram[:, 0:F0, :]
        w1t = prod[0:SPT * F0, 0:2, :].rearrange("p a n -> p (a n)")[:, 0:NK * M].rearrange("p (k m) -> p k m", m=M)
        sum1 = sb("sum1", [M, NCH, CH])
        sum2 = sb("sum2", [M, CH])
        s3 = sb("s3", [M, CH])
        denseT = sb("denseT", [D, B])
        wt1 = sb("wt1", [128, 3, 512])
        wt1d = sb("wt1d", [D, 512])
        bt1 = sb("bt1", [128, 4])
        wt2 = sb("wt2", [128, 4, 256])
        bt2 = sb("bt2", [128, 2])
        wt3 = sb("wt3", [128, 2])
        h1 = sb("h1", [128, 4, CH])
        h2 = sb("h2", [128, 2, CH])
        y = sb("y", [1, B])
        ident = sb("ident", [128, 128])
        rowmask = sb("rowmask", [128, TB])
        warm = sb("warm", [128, 1])

        ybank = [ctx.enter_context(nc.psum_tensor(f"ybank{i}", [128, 512], fp32)) for i in range(RING)]
        aux = [ctx.enter_context(nc.psum_tensor(f"aux{i}", [128, 512], fp32)) for i in range(2)]
        gbank = ctx.enter_context(nc.psum_tensor("gbank", [128, 512], fp32))

        w1_in, w2_in, w3_in, top_in = sem("w1_in"), sem("w2_in"), sem("w3_in"), sem("top_in")
        ids_in = sem("ids_in")
        rows_in = sem("rows_in")
        rows_tripled = sem("rows_tripled")
        const_step = sem("const_step")
        w1_ready = sem("w1_ready")
        x0rep_ready = sem("x0rep_ready")
        shifted_in = [[sem(f"shifted_in{p}_{k}") for k in range(NK)] for p in range(2)]
        pairs_ready = sem("pairs_ready")
        pairs0_ready = sem("pairs0_ready")
        x0pos_ready = sem("x0pos_ready")
        diag_ready = sem("diag_ready")
        w2h_ready, w2l_ready = sem("w2h_ready"), sem("w2l_ready")
        x1h_ready = sem("x1h_ready")
        x1_ready = sem("x1_ready")
        y_ready = sem("y_ready")
        prod_ready = sem("prod_ready")
        acc_step = sem("acc_step")
        joined = sem("joined")
        folded = sem("folded")
        x2_ready = sem("x2_ready")
        gram_ready = sem("gram_ready")
        gram_drained = sem("gram_drained")
        aux_full = sem("aux_full")
        aux_drained = [sem("aux_drained0"), sem("aux_drained1")]
        out_done = sem("out_done")
        CONSTS = 7

        block = ctx.enter_context(nc.Block())

        def pairs_count(c, g, k):
            return c * (NG * NK) + ((g - NG) * NK + k + 1)

        def shifted_count(c, g, k):
            return c * (NG // 2 * 16 * len(PAIR_TILES[k])) + (g // 2 + 1) * 16 * len(PAIR_TILES[k])

        @block.sync
        def _(sp):
            for c in range(2):
                sp.dma_start(row_ids[:, c, :], t["ids"][c * CH:(c + 1) * CH, :]).then_inc(ids_in, 16)
            sp.dma_start(w1[:, 0:NK - 1, :], t["w1a"][0:(NK - 1) * SPT * F0, :]
                         .rearrange("(k p) m -> p k m", p=SPT * F0)).then_inc(w1_in, 16)
            sp.dma_start(w1[0:2 * F0, NK - 1, :], t["w1a"][(NK - 1) * SPT * F0:, :]).then_inc(w1_in, 16)
            sp.dma_start(w1t[:, 0:NK - 1, :], t["w1b"][0:(NK - 1) * SPT * F0, :]
                         .rearrange("(k p) m -> p k m", p=SPT * F0)).then_inc(w1_in, 16)
            sp.dma_start(w1t[0:F0, NK - 1, :], t["w1b"][(NK - 1) * SPT * F0:, :]).then_inc(w1_in, 16)

            def shift(c, g):
                if g == 0:
                    sp.wait_ge(x0rep_ready, c + 1)
                if not zero(c) or g >= 2:
                    sp.wait_ge(x1_ready, c * NG + (g - 1))
                for k, shifts in enumerate(PAIR_TILES):
                    for j, s in enumerate(shifts):
                        sp.dma_start(pairs[j * F0:(j + 1) * F0, g % 2, k, :],
                                     x0rep[s:s + F0, g * GB:(g + 1) * GB, :].rearrange("p b d -> p (b d)")
                                     ).then_inc(shifted_in[g % 2][k], 16)

            def next_ids(c):
                sp.wait_ge(rows_in, c * (16 * F0))
                sp.dma_start(row_ids[:, 1, :], t["ids"][bass.ds(c * CH, CH), :]).then_inc(ids_in, 16)

            for g in range(NG):
                shift(0, g)
            with sp.Fori(1, NCH - 1) as c:
                for g in range(NG):
                    if g == 0:
                        next_ids(c + 1)
                    shift(c, g)
            for g in range(NG):
                shift(NCH - 1, g)
            last_use = (BASE + events(False, True)[1] + len(TAIL) - 1, NCH - 1)
            sp.wait_ge(aux_drained[bank_of(last_use)], taken_out(last_use))
            sp.dma_start(t["out"].rearrange("b o -> o b"), y[:]).then_inc(out_done, 16)
            sp.wait_ge(out_done, 16)

        @block.gpsimd
        def _(pool):
            nc.gpsimd.memset(ident[:], 0.0).then_inc(const_step, 1)
            nc.gpsimd.memset(rowmask[:], 1.0).then_inc(const_step, 1)
            nc.gpsimd.memset(x0pos[:, :, F0:FP], 1.0).then_inc(const_step, 1)
            nc.gpsimd.memset(warm[:], 0.0).then_inc(const_step, 1)
            pool.wait_ge(const_step, 4)
            nc.gpsimd.affine_select(out=ident[:], in_=ident[:], compare_op=ALU.not_equal, fill=1.0, base=0,
                                    pattern=[[-1, 128]], channel_multiplier=1).then_inc(const_step, 1)
            nc.gpsimd.affine_select(out=rowmask[:], in_=rowmask[:], compare_op=ALU.is_ge, fill=0.0, base=0,
                                    pattern=[[-D, TB]], channel_multiplier=1).then_inc(const_step, 1)
            pool.wait_ge(const_step, 6)
            nc.gpsimd.affine_select(out=rowmask[:], in_=rowmask[:], compare_op=ALU.is_ge, fill=0.0, base=D - 1,
                                    pattern=[[D, TB]], channel_multiplier=-1).then_inc(const_step, 1)
            pool.wait_ge(const_step, CONSTS)

            def gather(slot, features):
                for f in features:
                    nc.gpsimd.indirect_dma_start(
                        rows1[:, f, :], None, t["tables"][f],
                        bass.IndirectOffsetOnAxis(ap=row_ids[:, slot, f:f + 1].bitcast(u32), axis=0)
                        ).then_inc(rows_in, 16)

            def multiply_pairs(c, g, tiles):
                for k in tiles:
                    shifts = PAIR_TILES[k]
                    n = F0 * len(shifts)
                    pool.wait_ge(shifted_in[g % 2][k], shifted_count(c, g, k))
                    nc.gpsimd.tensor_tensor(pairs[0:n, g % 2, k, :], pairs[0:n, g % 2, k, :],
                                            x0rep[0:n, g * GB:(g + 1) * GB, :].rearrange("p b d -> p (b d)"),
                                            ALU.mult).then_inc(pairs_ready, 1)

            def spread_x0(c, g):
                if not zero(c) or g >= 2:
                    pool.wait_ge(gram_ready, c * TPC + ((g - 1) * GT + TPC))
                pool.wait_ge(x0pos_ready, c * NG + (g + 1))
                for i in range(GT):
                    last = nc.gpsimd.tensor_tensor(
                        x0diag[:, g % 2, i, :, :], x0pos[:, g * GT + i, :].unsqueeze(1).broadcast_to([128, TB, FP]),
                        rowmask[:].unsqueeze(2).broadcast_to([128, TB, FP]), ALU.mult)
                last.then_inc(diag_ready, 1)

            def fold(c, tt):
                slot = tt % 2
                done = c * TPC + tt
                pool.wait_ge(acc_step, c * (TPC * NSTEPS) + (tt + 2) * NSTEPS)
                nc.gpsimd.tensor_tensor(both[:], scaled[:, slot, :], added[:, slot, :], ALU.add).then_inc(joined, 1)
                pool.wait_ge(joined, done + 3)
                nc.gpsimd.tensor_tensor(both[:, 0:256], both[:, 0:256], both[:, 256:512], ALU.add).then_inc(folded, 1)
                pool.wait_ge(folded, done + 1)
                pool.wait_ge(gram_ready, done + (TPC - GT + 1))
                nc.gpsimd.tensor_tensor(x2[:, tt % GT, :], both[:, 0:128], both[:, 128:256],
                                        ALU.add).then_inc(x2_ready, 1)

            pool.sem_inc(joined, 2)
            pool.wait_ge(ids_in, 32)
            gather(0, range(F0))
            pool.wait_ge(rows_tripled, SPT)
            gather(1, range(F0))
            spread_x0(0, 0)

            gathered = [1, 2, 1, 6]
            taken = [sum(gathered[:i % GT]) + i // GT * sum(gathered) for i in range(TPC + 1)]
            taken = [min(n, F0) for n in taken]
            assert taken[-1] == F0

            def chunk(c, gathers, last):
                for tt in range(TPC):
                    g, i = tt // GT, tt % GT
                    if tt == 1 and gathers:
                        pool.wait_ge(ids_in, c * 16 + 48)
                        pool.wait_ge(rows_tripled, (c + 2) * SPT)
                    fold(c, tt)
                    if i == 0 and g + 1 < NG:
                        spread_x0(c, g + 1)
                    elif i == 0 and not last:
                        spread_x0(c + 1, 0)
                    if i == 1 and not last:
                        multiply_pairs(c + 1, g, range(NK // 2))
                    if i == 2 and not last:
                        multiply_pairs(c + 1, g, range(NK // 2, NK))
                    if gathers and tt > 0:
                        gather(1, range(taken[tt] if tt > 1 else 0, taken[tt + 1]))

            with pool.Fori(0, NCH - 2) as c:
                chunk(c, True, False)
            chunk(NCH - 2, False, False)
            chunk(NCH - 1, False, True)

        @block.tensor
        def _(pe):
            def take_aux(use):
                if not (zero(use[1]) and use[0] < 2):
                    pe.wait_ge(aux_drained[bank_of(use)], free_before(use))
                return aux[bank_of(use)]

            def wait_use(use):
                pe.wait_ge(aux_drained[bank_of(use)], taken_out(use))

            def x0_transposed(c, g, use):
                pe.wait_ge(rows_tripled, (c + 1) * SPT)
                for u in range(X0T_USES):
                    bank = take_aux((use[0] + u, use[1]))
                    for j in range(4):
                        last = nc.tensor.transpose(bank[0:SPT * F0, j * CH:(j + 1) * CH],
                                                   rows[:, :, 4 * u + j], ident[:])
                    last.then_inc(aux_full, 1)

            def wait_positions(c, use):
                pe.wait_ge(x0rep_ready, c + 1)
                pe.wait_ge(aux_drained[bank_of(use)], free_before(use))

            def x0_positions(c, g, use):
                for i in range(GT):
                    tt = g * GT + i
                    last = nc.tensor.transpose(
                        aux[bank_of(use)][:, i * FP:i * FP + F0],
                        x0rep[0:F0, tt * TB:(tt + 1) * TB, :].rearrange("p b d -> p (b d)"), ident[0:F0, 0:F0])
                last.then_inc(aux_full, 1)

            def layer1(c, g, use):
                bank = take_aux(use)
                for k, shifts in enumerate(PAIR_TILES):
                    n = F0 * len(shifts)
                    if zero(c):
                        pe.wait_ge(pairs0_ready, g * NK + k + 1)
                    else:
                        pe.wait_ge(pairs_ready, pairs_count(c, g, k))
                    last = nc.tensor.matmul(bank[:], w1[0:n, k, :], pairs[0:n, g % 2, k, :],
                                            start=(k == 0), stop=(k == NK - 1))
                last.then_inc(aux_full, 1)

            def gram_product(c, tt):
                g, i = tt // GT, tt % GT
                if i == 0:
                    pe.wait_ge(diag_ready, c * NG + (g + 1))
                pe.wait_ge(x2_ready, c * TPC + (tt + 1))
                pe.wait_ge(gram_drained, c * TPC + (tt + 1))
                nc.tensor.matmul(gbank[:, 0:TB * FP], x2[:, i, :],
                                 x0diag[:, g % 2, i, :, :].rearrange("p r f -> p (r f)"),
                                 start=True, stop=True).then_inc(gram_ready, 1)

            def tile(c, tt):
                if tt % GT == 0:
                    pe.wait_ge(x1_ready, c * NG + (tt // GT + 1))
                for q, feats in enumerate(GROUPS):
                    before, back = (q - RING, 1) if q >= RING else (q - RING + NQ, 0)
                    if before in ACT_Q:
                        pe.wait_ge(prod_ready, c * (TPC * NA) + ((tt + back) * NA + ACT_Q.index(before) + 1))
                    else:
                        pe.wait_ge(acc_step, c * (TPC * NSTEPS) + ((tt + back) * NSTEPS + step_of(before) + 1))
                    n = len(feats) * M
                    out = ybank[q % RING][:, 0:n]
                    pos = slice(tt * 128, (tt + 1) * 128)
                    high = w2h[:, feats[0]:feats[-1] + 1, :].rearrange("p f m -> p (f m)")
                    low = w2l[:, feats[0]:feats[-1] + 1, :].rearrange("p f m -> p (f m)")
                    nc.tensor.matmul(out, x1h[:, pos], high, start=True, stop=False)
                    nc.tensor.matmul(out, x1h[:, pos], low, start=False, stop=False)
                    nc.tensor.matmul(out, x1l[:, pos], high, start=False, stop=True).then_inc(y_ready, 1)
                    if q == GRAM_AFTER and not (zero(c) and tt == 0):
                        gram_product(c, tt - 1)

            def layer3(c, g, use):
                pe.wait_ge(gram_drained, (c + 1) * TPC + 1)
                bank = take_aux(use)
                for f in range(F0):
                    last = nc.tensor.matmul(bank[:, 0:CH], w3[:, f, :], gram[:, f, :],
                                            start=(f == 0), stop=(f == F0 - 1))
                last.then_inc(aux_full, 1)

            def mlp1(c, g, use, before):
                wait_use(before)
                bank = take_aux(use)
                for i in range(4):
                    cols = slice(i * 128, (i + 1) * 128)
                    nc.tensor.matmul(bank[:, cols], wt1[:, 1, cols], sum2[:], start=True, stop=False)
                    nc.tensor.matmul(bank[:, cols], wt1[:, 0, cols],
                                     sum1[:, bass.ds(c, 1), :].rearrange("p c b -> p (c b)"), start=False, stop=False)
                    nc.tensor.matmul(bank[:, cols], wt1[:, 2, cols], s3[:], start=False, stop=False)
                    last = nc.tensor.matmul(bank[:, cols], wt1d[:, cols], denseT[:, bass.ds(c * CH, CH)],
                                            start=False, stop=True)
                last.then_inc(aux_full, 1)

            def mlp2(c, g, use, before):
                wait_use(before)
                bank = take_aux(use)
                for i in range(2):
                    for k in range(4):
                        last = nc.tensor.matmul(bank[:, i * CH:(i + 1) * CH], wt2[:, k, i * 128:(i + 1) * 128],
                                                h1[:, k, :], start=(k == 0), stop=(k == 3))
                last.then_inc(aux_full, 1)

            def mlp3(c, g, use, before):
                wait_use(before)
                bank = take_aux(use)
                for k in range(2):
                    last = nc.tensor.matmul(bank[0:1, 0:CH], wt3[:, k:k + 1], h2[:, k, :],
                                            start=(k == 0), stop=(k == 1))
                last.then_inc(aux_full, 1)

            prep = {"x0T": x0_transposed, "x0P": x0_positions, "layer1": layer1}
            mlp = {"mlp1": mlp1, "mlp2": mlp2, "mlp3": mlp3}

            pe.sem_inc(gram_ready, TPC)
            pe.wait_ge(const_step, CONSTS)
            pe.wait_ge(w1_ready, 2)
            use = (0, 0)
            for what, g in PROLOGUE:
                if what == "x0P":
                    wait_positions(0, use)
                prep[what](0, g, use)
                use = (use[0] + uses_of(what), 0)
            pe.wait_ge(w2h_ready, 1)
            pe.wait_ge(w2l_ready, 1)
            pe.wait_ge(w3_in, 16)
            pe.wait_ge(top_in, 16 * 7)

            def chunk(c, first, last):
                todo, _ = events(first, last)
                base = (USES0, 0) if first else (BASE, c)
                tail_use = None
                for tt in range(TPC):
                    for after, what, g, n in todo:
                        if after == tt and what == "x0P":
                            back = g == NG - 1
                            if not back:
                                wait_positions(c + 1, (base[0] + n - 0, base[1]))
                    tile(c, tt)
                    for after, what, g, n in todo:
                        use = (base[0] + n, base[1])
                        if after != tt:
                            continue
                        if what == "layer3":
                            layer3(c - 1, g, use)
                            tail_use = use
                        elif what in mlp:
                            mlp[what](c - 1, g, use, tail_use)
                            tail_use = use
                        elif what == "x0P" and g == NG - 1:
                            x0_positions(c, g, use)
                        else:
                            prep[what](c + 1, g, use)

            def finish(c):
                gram_product(c, TPC - 1)
                use = (BASE + events(False, True)[1], c)
                layer3(c, 0, use)
                for what in TAIL[1:]:
                    before, use = use, (use[0] + 1, c)
                    mlp[what](c, 0, use, before)

            chunk(0, True, False)
            with pe.Fori(1, NCH - 1) as c:
                chunk(c, False, False)
            chunk(NCH - 1, False, True)
            finish(NCH - 1)

        @block.scalar
        def _(act):
            act.dma_start(w2raw, t["f1"].rearrange("(f g) m -> g f m", g=M)).then_inc(w2_in, 16)
            act.dma_start(w3[:], t["f2"].rearrange("(f g) m -> g f m", g=M)).then_inc(w3_in, 16)
            act.dma_start(wt1[:], t["wt1"][0:384, :].rearrange("(k p) n -> p k n", p=128)).then_inc(top_in, 16)
            act.dma_start(wt1d[:], t["wt1"][384:400, :]).then_inc(top_in, 16)
            act.dma_start(wt2[:], t["wt2"].rearrange("(k p) n -> p k n", p=128)).then_inc(top_in, 16)
            act.dma_start(bt1[:], t["bt1"]).then_inc(top_in, 16)
            act.dma_start(bt2[:], t["bt2"]).then_inc(top_in, 16)
            act.dma_start(wt3[:], t["wt3"]).then_inc(top_in, 16)
            act.dma_start(denseT[:], t["denseT"]).then_inc(top_in, 16)
            act.wait_ge(const_step, CONSTS)
            nc.scalar.activation(warm[:], ident[:, 0:1], ACT.Copy)
            act.sem_inc(prod_ready, NA)
            act.sem_inc(gram_drained, 1)
            act.wait_ge(w2_in, 16)
            nc.scalar.copy(w2h[:], w2raw).then_inc(w2h_ready, 1)

            def x0_transposed(c, g, use):
                act.wait_ge(rows_in, (c + 1) * (16 * F0))
                for j in range(SPT):
                    nc.scalar.copy(rows[:, j * F0:(j + 1) * F0, :], rows1[:]).then_inc(rows_tripled, 1)
                if isinstance(c, int) and c == 1:
                    act.wait_ge(pairs0_ready, NG * NK)
                elif not isinstance(c, int):
                    act.wait_ge(pairs_ready, pairs_count(c - 1, NG - 1, NK - 1))
                for u in range(X0T_USES):
                    now = (use[0] + u, use[1])
                    act.wait_ge(aux_full, filled(now))
                    nc.scalar.copy(x0rep[:, :, 4 * u:4 * (u + 1)].rearrange("p b d -> p d b"),
                                   aux[bank_of(now)][0:SPT * F0, :].rearrange("p (d b) -> p d b", d=4)
                                   ).then_inc(aux_drained[bank_of(now)], 1)
                for now in ((use[0] + X0T_USES - 2, use[1]), (use[0] + X0T_USES - 1, use[1])):
                    act.wait_ge(aux_drained[bank_of(now)], taken_out(now))
                act.sem_inc(x0rep_ready, 1)

            def x0_positions(c, g, use):
                if not zero(c):
                    act.wait_ge(x2_ready, c * TPC + ((g + 1) * GT - TPC))
                    act.wait_ge(diag_ready, c * NG + (g + 1 - NG))
                act.wait_ge(aux_full, filled(use))
                nc.scalar.copy(x0pos[:, g * GT:(g + 1) * GT, 0:F0],
                               aux[bank_of(use)][:, 0:GT * FP].rearrange("p (t f) -> p t f", f=FP)[:, :, 0:F0]
                               ).then_inc(aux_drained[bank_of(use)], 1)
                act.wait_ge(aux_drained[bank_of(use)], taken_out(use))
                act.sem_inc(x0pos_ready, 1)

            def layer1(c, g, use):
                act.wait_ge(aux_full, filled(use))
                nc.scalar.copy(x1h[:, 512 * g:512 * (g + 1)], aux[bank_of(use)][:]).then_inc(x1h_ready, 1)

            def gram_out(c, tt):
                act.wait_ge(gram_ready, c * TPC + tt + (TPC + 1))
                col = (TPC - 1) * TB if isinstance(tt, int) and tt < 0 else tt * TB
                nc.scalar.copy(gram[:, :, bass.ds(col, TB)].rearrange("p f r -> p r f"),
                               gbank[:, 0:TB * FP].rearrange("p (r f) -> p r f", f=FP)).then_inc(gram_drained, 1)

            def tile(c, tt, with_gram):
                for i, q in enumerate(ACT_Q):
                    ahead = NSTEPS if i >= PRODS else 0
                    act.wait_ge(acc_step, c * (TPC * NSTEPS) + tt * NSTEPS + (ahead + step_of(ACT_Q[(i - PRODS) % NA]) + 1))
                    act.wait_ge(y_ready, c * (TPC * NQ) + tt * NQ + (q + 1))
                    for j, f in enumerate(GROUPS[q]):
                        last = nc.scalar.activation(prod[:, i % PRODS, j * M:(j + 1) * M],
                                                    ybank[q % RING][:, j * M:(j + 1) * M], ACT.Copy,
                                                    scale=x0pos[:, bass.ds(tt, 1), f:f + 1].rearrange("p t f -> p (t f)"))
                    last.then_inc(prod_ready, 1)
                    if q == GRAM_AFTER and with_gram:
                        gram_out(c, tt - 1)

            def layer3(c, g, use):
                act.wait_ge(aux_full, filled(use))
                nc.scalar.copy(sum2[:], gram[:, F0, :])
                nc.scalar.copy(s3[:], aux[bank_of(use)][:, 0:CH]).then_inc(aux_drained[bank_of(use)], 1)

            def mlp1(c, g, use):
                act.wait_ge(aux_full, filled(use))
                for i in range(4):
                    last = nc.scalar.activation(h1[:, i, :], aux[bank_of(use)][:, i * CH:(i + 1) * CH], ACT.Relu,
                                                bias=bt1[:, i:i + 1])
                last.then_inc(aux_drained[bank_of(use)], 1)

            def mlp2(c, g, use):
                act.wait_ge(aux_full, filled(use))
                for i in range(2):
                    last = nc.scalar.activation(h2[:, i, :], aux[bank_of(use)][:, i * CH:(i + 1) * CH], ACT.Relu,
                                                bias=bt2[:, i:i + 1])
                last.then_inc(aux_drained[bank_of(use)], 1)

            def mlp3(c, g, use):
                act.wait_ge(aux_full, filled(use))
                nc.scalar.copy(y[:, bass.ds(c * CH, CH)],
                               aux[bank_of(use)][0:1, 0:CH]).then_inc(aux_drained[bank_of(use)], 1)

            prep = {"x0T": x0_transposed, "x0P": x0_positions, "layer1": layer1}
            tail = {"layer3": layer3, "mlp1": mlp1, "mlp2": mlp2, "mlp3": mlp3}

            use = (0, 0)
            for what, g in PROLOGUE:
                prep[what](0, g, use)
                use = (use[0] + uses_of(what), 0)
            act.wait_ge(top_in, 16 * 7)

            def chunk(c, first, last):
                todo, _ = events(first, last)
                base = (USES0, 0) if first else (BASE, c)
                tt = 0
                while tt < TPC:
                    if tt % GT == 0:
                        act.wait_ge(x0pos_ready, c * NG + (tt // GT + 1))
                    stop = min([after for after, *_ in todo if after >= tt] + [(tt // GT + 1) * GT - 1]) + 1
                    if stop - tt == 1 or tt == 0:
                        tile(c, tt, not (first and tt == 0))
                        stop = tt + 1
                    else:
                        with act.Fori(tt, stop) as i:
                            tile(c, i, True)
                    for after, what, g, n in todo:
                        use = (base[0] + n, base[1])
                        if after != stop - 1:
                            continue
                        if what in tail:
                            tail[what](c - 1, g, use)
                        else:
                            prep[what](c if (what, g) == ("x0P", NG - 1) else c + 1, g, use)
                    tt = stop

            def finish(c):
                gram_out(c, TPC - 1)
                use = (BASE + events(False, True)[1], c)
                for what in TAIL:
                    tail[what](c, 0, use)
                    use = (use[0] + 1, c)

            chunk(0, True, False)
            with act.Fori(1, NCH - 1) as c:
                chunk(c, False, False)
            chunk(NCH - 1, False, True)
            finish(NCH - 1)

        @block.vector
        def _(dve):
            dve.sem_inc(acc_step, NSTEPS)
            dve.wait_ge(w1_in, 16 * 4)
            nc.vector.tensor_tensor(w1[:, 0:NK - 1, :], w1[:, 0:NK - 1, :], w1t[:, 0:NK - 1, :],
                                    ALU.add).then_inc(w1_ready, 1)
            nc.vector.tensor_tensor(w1[0:F0, NK - 1, :], w1[0:F0, NK - 1, :], w1t[0:F0, NK - 1, :],
                                    ALU.add).then_inc(w1_ready, 1)
            dve.wait_ge(w2h_ready, 1)
            nc.vector.tensor_tensor(w2l[:], w2raw, w2h[:].bitcast(fp32), ALU.subtract).then_inc(w2l_ready, 1)

            def first_pairs(g):
                for k, shifts in enumerate(PAIR_TILES):
                    n = F0 * len(shifts)
                    dve.wait_ge(shifted_in[g % 2][k], shifted_count(0, g, k))
                    nc.vector.tensor_tensor(pairs[0:n, g % 2, k, :], pairs[0:n, g % 2, k, :],
                                            x0rep[0:n, g * GB:(g + 1) * GB, :].rearrange("p b d -> p (b d)"),
                                            ALU.mult).then_inc(pairs0_ready, 1)

            def layer1(c, g, use):
                cols = slice(512 * g, 512 * (g + 1))
                dve.wait_ge(x1h_ready, c * NG + (g + 1))
                bank = aux[bank_of(use)]
                nc.vector.tensor_tensor(x1l[:, cols], bank[:], x1h[:, cols].bitcast(fp32),
                                        ALU.subtract).then_inc(x1_ready, 1)
                nc.vector.tensor_reduce(sum1[:, bass.ds(c, 1), g * GB:(g + 1) * GB].rearrange("p c b -> p (c b)"),
                                        bank[:].rearrange("p (b d) -> p b d", d=D), AX.X,
                                        ALU.add).then_inc(aux_drained[bank_of(use)], 1)

            uses1 = {g: (X0T_USES + NG - 1 + g, 0) for g in range(NG)}
            first_pairs(0)
            for g in range(NG):
                if g + 1 < NG:
                    first_pairs(g + 1)
                layer1(0, g, uses1[g])

            def group(c, g):
                with dve.Fori(g * GT // 2, (g + 1) * GT // 2) as pair:
                    for slot in range(2):
                        tile(c, g, pair * 2 + slot, slot)

            def tile(c, g, tt, slot):
                done = c * (TPC * NSTEPS) + (tt + 1) * NSTEPS
                groups = c * (TPC * NQ) + tt * NQ
                products = c * (TPC * NA) + (tt + 1) * NA

                dve.wait_ge(x0pos_ready, c * NG + (g + 1))

                def product(q):
                    i = ACT_Q.index(q)
                    dve.wait_ge(prod_ready, products + (i + 1))
                    return prod[:, i % PRODS, :]

                dve.wait_ge(joined, c * TPC + tt + 1)
                for i, (kind, used) in enumerate(STEPS):
                    if step_before(i):
                        dve.wait_ge(acc_step, done + step_before(i))
                    if kind == "scale":
                        q = used[0]
                        start = product(used[1]) if len(used) > 1 else scaled[:, slot, :]
                        dve.wait_ge(y_ready, groups + (q + 1))
                        for j, f in enumerate(GROUPS[q]):
                            cols = slice(j * M, (j + 1) * M)
                            last = nc.vector.scalar_tensor_tensor(
                                out=scaled[:, slot, cols], in0=ybank[q % RING][:, cols],
                                scalar=x0pos[:, bass.ds(tt, 1), f:f + 1].rearrange("p t f -> p (t f)"),
                                in1=start[:, cols], op0=ALU.mult, op1=ALU.add)
                    else:
                        terms = [product(q) for q in used]
                        last = nc.vector.tensor_tensor(
                            added[:, slot, :], terms[0], terms[1] if len(terms) > 1 else added[:, slot, :], ALU.add)
                    last.then_inc(acc_step, 1)

            def chunk(c, first, last):
                base = (USES0, 0) if first else (BASE, c)
                uses = {g: (base[0] + n, base[1]) for _, what, g, n in events(first, last)[0] if what == "layer1"}
                for g in range(NG):
                    group(c, g)
                    if not last:
                        layer1(c + 1, g, uses[g])

            chunk(0, True, False)
            with dve.Fori(1, NCH - 1) as c:
                chunk(c, False, False)
            chunk(NCH - 1, False, True)


def pair_rows():
    fg = [(f, (f + s) % F0) for s in SHIFTS for f in range(F0)]
    return [f * F0 + g for f, g in fg], [g * F0 + f for f, g in fg[:(NS - 1) * F0]]


def kernel(**inputs):
    import numpy as np
    import concourse.bacc as bacc
    from concourse.bass_utils import run_bass_kernel_spmd

    nc = bacc.Bacc("TRN2", target_bir_lowering=False, num_devices=1)
    arrays = {}

    def dram(name, a):
        a = np.ascontiguousarray(a)
        name = f"in_{name}"
        arrays[name] = a
        return nc.dram_tensor(name, a.shape, mybir.dt.from_np(a.dtype), kind="ExternalInput").ap()

    first, second = pair_rows()
    f0 = np.asarray(inputs["L0_rec_f0"])
    t = {
        "ids": dram("ids", inputs["ids"]),
        "tables": [dram(f"table{f}", inputs[f"tbl_{f}"]) for f in range(F0)],
        "w1a": dram("w1a", f0[first]),
        "w1b": dram("w1b", f0[second]),
        "f1": dram("f1", inputs["L0_rec_f1"]),
        "f2": dram("f2", inputs["L0_rec_f2"]),
        "denseT": dram("denseT", np.asarray(inputs["dense_ctx"]).T),
        "wt1": dram("wt1", inputs["W_top1"]),
        "wt2": dram("wt2", inputs["W_top2"]),
        "bt1": dram("bt1", np.asarray(inputs["b_top1"]).reshape(4, 128).T),
        "bt2": dram("bt2", np.asarray(inputs["b_top2"]).reshape(2, 128).T),
        "wt3": dram("wt3", np.asarray(inputs["W_top3"]).reshape(2, 128).T),
        "out": nc.dram_tensor("out", (B, 1), mybir.dt.float32, kind="ExternalOutput").ap(),
    }
    build(nc, t)
    r = run_bass_kernel_spmd(nc, [arrays], core_ids=[0])
    return r.results[0]["out"]
```

```python
import concourse.bass as bass
from concourse import mybir
from contextlib import ExitStack

B, F0, D, M = 512, 39, 16, 128
CH = 128
NCH = B // CH
TB = 128 // D
TPC = CH // TB
POS = CH * D
FP = F0 + 1
NS = (F0 + 1) // 2
SPT = 3
NK = -(-NS // SPT)
PAIR_ROWS = [F0 * len(range(k, NS, NK)) for k in range(NK)]
FACTOR_START = [-NK * j % F0 for j in range(SPT)]
PER = SPT * F0 + NK - 1
LATE = 7
NG = POS // 512
GT = TPC // NG
GB = CH // NG

GROUPS = [list(range(f, min(f + 4, F0))) for f in range(0, F0, 4)]
NQ = len(GROUPS)
RING = 5
ACT_Q = [0, 2, 3, 5, 6, 8]
DVE_Q = [q for q in range(NQ) if q not in ACT_Q]
NA = len(ACT_Q)
PRODS = 3
GRAM_AFTER = 8
STEPS = [("scale", [1, 0]), ("scale", [4]), ("add", [2, 3]), ("add", [5]), ("scale", [7]),
         ("add", [6]), ("scale", [9]), ("add", [8])]
NSTEPS = len(STEPS)


def step_of(q):
    return next(i for i, (_, used) in enumerate(STEPS) if q in used)


def step_before(i):
    earlier = [n for n in range(i) if STEPS[n][0] == STEPS[i][0]]
    return earlier[-1] + 1 if earlier else 0


EVENTS = [(0, "x0P", NG - 1), (0, "x0T", 0), (0, "layer3", 0), (1, "mlp1", 0), (2, "mlp2", 0), (3, "mlp3", 0),
          (5, "layer1", 0), (6, "x0P", 0), (9, "layer1", 1), (10, "x0P", 1), (13, "layer1", 2), (14, "x0P", 2),
          (15, "early rows", 2), (15, "late rows", 2), (15, "layer1", 3)]
FIRST_EVENTS = [(0, "x0P", NG - 1), (0, "early rows", 1), (1, "late rows", 1), (1, "x0T", 0)] \
    + [e for e in EVENTS if e[0] > 0]
COPIES = ["early rows", "late rows"]
TAIL = ["layer3", "mlp1", "mlp2", "mlp3"]
X0T_USES = D // 4
PROLOGUE = [("x0T", 0)] + [("x0P", g) for g in range(NG - 1)] + [("layer1", g) for g in range(NG)]
PROLOGUE_LAYER1 = X0T_USES + NG - 1

VPAIRS = 3
PPAIRS = NK - VPAIRS
VPAIRS_AFTER = {1: [0], 5: [1], 9: [2], 13: [3]}
FIRST_VPAIRS_AFTER = {5: [0, 1], 9: [2], 13: [3]}
PPAIRS_AFTER = {3: (0, 3, 6), 4: (0, 6, 7), 6: (1, 3, 5), 7: (1, 5, 7), 10: (2, 3, 5), 11: (2, 5, 7), 14: (3, 3, 7)}
GATHERS = [10, 5, 3, 0, 0, 8, 1, 1, 1, 8, 1, 1, 0, 0, 0, 0]
FIRST_GATHERS = [0, 5, 4, 0, 0, 9, 2, 1, 1, 9, 2, 1, 1, 4, 0, 0]
assert sum(GATHERS) == sum(FIRST_GATHERS) == F0


def zero(c):
    return isinstance(c, int) and c == 0


def uses_of(what):
    return 0 if what in COPIES else X0T_USES if what == "x0T" else 1


def events(first, last):
    out, n = [], 0
    for tile, what, g in FIRST_EVENTS if first else EVENTS:
        if (first and what in TAIL) or (last and what not in TAIL and (what, g) != ("x0P", NG - 1)):
            continue
        out.append((tile, what, g, n))
        n += uses_of(what)
    return out, n


USES = events(False, False)[1]
USES0 = sum(uses_of(what) for what, _ in PROLOGUE)
BASE = USES0 + events(True, False)[1] - USES
assert USES % 2 == 0 and BASE > 0


def layer1_use(c, g):
    if zero(c):
        return (PROLOGUE_LAYER1 + g, 0)
    n = BASE - USES + next(n for _, what, group, n in events(False, False)[0] if (what, group) == ("layer1", g))
    assert n >= 0
    return (n, c)


def bank_of(use):
    return use[0] % 2


def filled(use):
    return use[1] * USES + (use[0] + 1)


def free_before(use):
    return use[1] * (USES // 2) + use[0] // 2


def taken_out(use):
    return use[1] * (USES // 2) + (use[0] // 2 + 1)


def build(nc, t):
    fp32, fp32r, i32, u32 = mybir.dt.float32, mybir.dt.float32r, mybir.dt.int32, mybir.dt.uint32
    ALU, ACT, AX = mybir.AluOpType, mybir.ActivationFunctionType, mybir.AxisListType
    ctx = ExitStack()
    with ctx:
        def sb(name, shape, dt=fp32):
            return ctx.enter_context(nc.sbuf_tensor(name, shape, dt))

        def sem(name):
            return ctx.enter_context(nc.semaphore(name))

        row_ids = sb("row_ids", [CH, 2, F0], i32)
        rows1 = sb("rows1", [CH, F0, D])
        rows = sb("rows", [CH, PER, D])
        x0per = sb("x0per", [PER, CH, D])
        factor = sb("factor", [SPT * F0, 2, 512])
        pairs = sb("pairs", [SPT * F0, 2, NK, 512])
        x0pos = sb("x0pos", [128, TPC, FP])
        x0diag = sb("x0diag", [128, 2, GT, TB, FP])
        x1h = sb("x1h", [M, POS], fp32r)
        x1l = sb("x1l", [M, POS], fp32r)
        w1 = sb("w1", [SPT * F0, NK, M])
        w2h = sb("w2h", [M, F0, M], fp32r)
        w2l = sb("w2l", [M, F0, M], fp32r)
        w3 = sb("w3", [M, F0, M])
        prod = sb("prod", [128, PRODS, 512])
        scaled = sb("scaled", [128, 2, 512])
        added = sb("added", [128, 2, 512])
        both = sb("both", [128, 512])
        x2 = sb("x2", [128, GT, M])
        gram = sb("gram", [M, FP, CH])
        periods = rows[:, 0:SPT * F0, :].rearrange("p (j f) d -> p j f d", f=F0)
        EARLY_F, LATE_F = slice(0, F0 - LATE), slice(F0 - LATE, F0)
        w2raw = gram[:, 0:F0, :]
        w1t = prod[0:SPT * F0, 0:2, :].rearrange("p a n -> p (a n)")[:, 0:NK * M].rearrange("p (k m) -> p k m", m=M)
        sum1 = sb("sum1", [M, NCH, CH])
        sum2 = sb("sum2", [M, CH])
        s3 = sb("s3", [M, CH])
        denseT = sb("denseT", [D, B])
        wt1 = sb("wt1", [128, 3, 512])
        wt1d = sb("wt1d", [D, 512])
        bt1 = sb("bt1", [128, 4])
        wt2 = sb("wt2", [128, 4, 256])
        bt2 = sb("bt2", [128, 2])
        wt3 = sb("wt3", [128, 2])
        h1 = sb("h1", [128, 4, CH])
        h2 = sb("h2", [128, 2, CH])
        y = sb("y", [1, B])
        ident = sb("ident", [128, 128])
        rowmask = sb("rowmask", [128, TB])

        ybank = [ctx.enter_context(nc.psum_tensor(f"ybank{i}", [128, 512], fp32)) for i in range(RING)]
        aux = [ctx.enter_context(nc.psum_tensor(f"aux{i}", [128, 512], fp32)) for i in range(2)]
        gbank = ctx.enter_context(nc.psum_tensor("gbank", [128, 512], fp32))

        w1_in, w2_in, w3_in, top_in = sem("w1_in"), sem("w2_in"), sem("w3_in"), sem("top_in")
        ids_in = sem("ids_in")
        next_ids_in = sem("next_ids_in")
        early_in, late_in = sem("early_in"), sem("late_in")
        rows_copied = sem("rows_copied")
        const_step = sem("const_step")
        w1_step = sem("w1_step")
        x0per_ready = sem("x0per_ready")
        factor_in = [sem("factor_in0"), sem("factor_in1")]
        shifted_in = [[sem(f"shifted_in{p}_{k}") for k in range(NK)] for p in range(2)]
        ppairs_ready = sem("ppairs_ready")
        vpairs_ready = sem("vpairs_ready")
        x0pos_ready = sem("x0pos_ready")
        diag_ready = sem("diag_ready")
        w2h_ready, w2l_ready = sem("w2h_ready"), sem("w2l_ready")
        x1h_ready = sem("x1h_ready")
        x1_ready = sem("x1_ready")
        y_ready = sem("y_ready")
        prod_ready = sem("prod_ready")
        acc_step = sem("acc_step")
        joined = sem("joined")
        folded = sem("folded")
        vfolded = sem("vfolded")
        x2_ready = sem("x2_ready")
        gram_ready = sem("gram_ready")
        gram_drained = sem("gram_drained")
        aux_full = sem("aux_full")
        aux_drained = [sem("aux_drained0"), sem("aux_drained1")]
        out_done = sem("out_done")
        CONSTS = 6

        block = ctx.enter_context(nc.Block())

        def multiplied(c, g, k):
            if zero(c):
                return vpairs_ready, g * NK + k + 1
            if k < VPAIRS:
                return vpairs_ready, c * (NG * VPAIRS) + (NG * (NK - VPAIRS) + g * VPAIRS + k + 1)
            return ppairs_ready, c * (NG * PPAIRS) + ((g - NG) * PPAIRS + k - VPAIRS + 1)

        def slot_count(c, g, dmas):
            return c * (NG // 2 * 16 * dmas) + (g // 2 + 1) * 16 * dmas

        @block.sync
        def _(sp):
            sp.dma_start(row_ids[:, 0, :], t["ids"][0:CH, :]).then_inc(ids_in, 16)
            sp.dma_start(w1[:], t["w1a"]).then_inc(w1_in, 16)
            sp.dma_start(w1t[:, 1:NK, :], t["w1b"][:, 1:NK, :]).then_inc(w1_in, 16)
            sp.dma_start(w1t[F0:, 0, :], t["w1b"][F0:, 0, :]).then_inc(w1_in, 16)
            sp.dma_start(row_ids[:, 1, :], t["ids"][CH:2 * CH, :]).then_inc(next_ids_in, 16)

            def shift(c, g):
                if g == 0:
                    sp.wait_ge(x0per_ready, c + 1)
                if g >= 2:
                    sp.wait_ge(aux_full, filled(layer1_use(c, g - 2)))
                elif not zero(c):
                    sp.wait_ge(x1_ready, c * NG + (g - 1))
                for j, start in enumerate(FACTOR_START):
                    sp.dma_start(factor[j * F0:(j + 1) * F0, g % 2, :],
                                 x0per[start:start + F0, g * GB:(g + 1) * GB, :].rearrange("p b d -> p (b d)")
                                 ).then_inc(factor_in[g % 2], 16)
                for k in range(1, NK):
                    sp.dma_start(pairs[0:PAIR_ROWS[k], g % 2, k, :],
                                 x0per[k:k + PAIR_ROWS[k], g * GB:(g + 1) * GB, :].rearrange("p b d -> p (b d)")
                                 ).then_inc(shifted_in[g % 2][k], 16)

            def next_ids(c):
                sp.wait_ge(rows_copied, c)
                sp.dma_start(row_ids[:, 1, :], t["ids"][bass.ds(c * CH, CH), :]).then_inc(next_ids_in, 16)

            for g in range(NG):
                shift(0, g)
            with sp.Fori(1, NCH - 1) as c:
                for g in range(NG):
                    if g == 0:
                        next_ids(c + 1)
                    shift(c, g)
            for g in range(NG):
                shift(NCH - 1, g)
            last_use = (BASE + events(False, True)[1] + len(TAIL) - 1, NCH - 1)
            sp.wait_ge(aux_drained[bank_of(last_use)], taken_out(last_use))
            sp.dma_start(t["out"].rearrange("b o -> o b"), y[:]).then_inc(out_done, 16)
            sp.wait_ge(out_done, 16)

        @block.gpsimd
        def _(pool):
            def gather(slot, features):
                for f in features:
                    nc.gpsimd.indirect_dma_start(
                        rows1[:, f, :], None, t["tables"][f],
                        bass.IndirectOffsetOnAxis(ap=row_ids[:, slot, f:f + 1].bitcast(u32), axis=0)
                        ).then_inc(early_in if f < F0 - LATE else late_in, 16)

            def multiply_pairs(c, g, start, stop):
                if start == VPAIRS:
                    pool.wait_ge(factor_in[g % 2], slot_count(c, g, SPT))
                for k in range(start, stop):
                    n = PAIR_ROWS[k]
                    pool.wait_ge(shifted_in[g % 2][k], slot_count(c, g, 1))
                    nc.gpsimd.tensor_tensor(pairs[0:n, g % 2, k, :], pairs[0:n, g % 2, k, :], factor[0:n, g % 2, :],
                                            ALU.mult).then_inc(ppairs_ready, 1)

            def spread_x0(c, g):
                if not zero(c) or g >= 2:
                    pool.wait_ge(gram_ready, c * TPC + ((g - 1) * GT + TPC))
                pool.wait_ge(x0pos_ready, c * NG + (g + 1))
                for i in range(GT):
                    last = nc.gpsimd.tensor_tensor(
                        x0diag[:, g % 2, i, :, :], x0pos[:, g * GT + i, :].unsqueeze(1).broadcast_to([128, TB, FP]),
                        rowmask[:].unsqueeze(2).broadcast_to([128, TB, FP]), ALU.mult)
                last.then_inc(diag_ready, 1)

            def fold(c, tt):
                slot = tt % 2
                done = c * TPC + tt
                pool.wait_ge(acc_step, c * (TPC * NSTEPS) + (tt + 2) * NSTEPS)
                nc.gpsimd.tensor_tensor(both[:], scaled[:, slot, :], added[:, slot, :], ALU.add).then_inc(joined, 1)
                pool.wait_ge(joined, done + 3)
                nc.gpsimd.tensor_tensor(both[:, 0:256], both[:, 0:256], both[:, 256:512], ALU.add).then_inc(folded, 1)
                pool.wait_ge(folded, done + 1)
                pool.wait_ge(gram_ready, done + (TPC - GT + 1))
                nc.gpsimd.tensor_tensor(x2[:, tt % GT, :], both[:, 0:128], both[:, 128:256],
                                        ALU.add).then_inc(x2_ready, 1)

            pool.sem_inc(joined, 2)
            pool.wait_ge(ids_in, 16)
            gather(0, range(F0))
            nc.gpsimd.memset(ident[:], 0.0).then_inc(const_step, 1)
            nc.gpsimd.memset(rowmask[:], 1.0).then_inc(const_step, 1)
            nc.gpsimd.memset(x0pos[:, :, F0:FP], 1.0).then_inc(const_step, 1)
            pool.wait_ge(const_step, 3)
            nc.gpsimd.affine_select(out=ident[:], in_=ident[:], compare_op=ALU.not_equal, fill=1.0, base=0,
                                    pattern=[[-1, 128]], channel_multiplier=1).then_inc(const_step, 1)
            nc.gpsimd.affine_select(out=rowmask[:], in_=rowmask[:], compare_op=ALU.is_ge, fill=0.0, base=0,
                                    pattern=[[-D, TB]], channel_multiplier=1).then_inc(const_step, 1)
            pool.wait_ge(const_step, 5)
            nc.gpsimd.affine_select(out=rowmask[:], in_=rowmask[:], compare_op=ALU.is_ge, fill=0.0, base=D - 1,
                                    pattern=[[D, TB]], channel_multiplier=-1).then_inc(const_step, 1)
            pool.wait_ge(const_step, CONSTS)
            pool.wait_ge(next_ids_in, 16)
            pool.wait_ge(rows_copied, 1)
            gather(1, range(F0))
            spread_x0(0, 0)

            def chunk(c, gathers, last):
                for tt in range(TPC - 1 if last else TPC):
                    g, i = tt // GT, tt % GT
                    if gathers[tt] and not any(gathers[:tt]):
                        pool.wait_ge(next_ids_in, c * 16 + 32)
                        pool.wait_ge(rows_copied, c + 2)
                    fold(c, tt)
                    if i == 0 and g + 1 < NG:
                        spread_x0(c, g + 1)
                    elif i == 0 and not last:
                        spread_x0(c + 1, 0)
                    if tt in PPAIRS_AFTER and not last:
                        multiply_pairs(c + 1, *PPAIRS_AFTER[tt])
                    if gathers[tt]:
                        gather(1, range(sum(gathers[:tt]), sum(gathers[:tt + 1])))

            chunk(0, FIRST_GATHERS, False)
            with pool.Fori(1, NCH - 2) as c:
                chunk(c, GATHERS, False)
            chunk(NCH - 2, [0] * TPC, False)
            chunk(NCH - 1, [0] * TPC, True)

        @block.tensor
        def _(pe):
            def take_aux(use):
                if not (zero(use[1]) and use[0] < 2):
                    pe.wait_ge(aux_drained[bank_of(use)], free_before(use))
                return aux[bank_of(use)]

            def wait_use(use):
                pe.wait_ge(aux_drained[bank_of(use)], taken_out(use))

            def x0_transposed(c, g, use):
                pe.wait_ge(rows_copied, c + 1)
                for u in range(X0T_USES):
                    bank = take_aux((use[0] + u, use[1]))
                    for j in range(4):
                        last = nc.tensor.transpose(bank[0:PER, j * CH:(j + 1) * CH],
                                                   rows[:, :, 4 * u + j], ident[:])
                    last.then_inc(aux_full, 1)

            def wait_positions(c, use):
                pe.wait_ge(x0per_ready, c + 1)
                pe.wait_ge(aux_drained[bank_of(use)], free_before(use))

            def x0_positions(c, g, use):
                for i in range(GT):
                    tt = g * GT + i
                    last = nc.tensor.transpose(
                        aux[bank_of(use)][:, i * FP:i * FP + F0],
                        x0per[0:F0, tt * TB:(tt + 1) * TB, :].rearrange("p b d -> p (b d)"), ident[0:F0, 0:F0])
                last.then_inc(aux_full, 1)

            def layer1(c, g, use):
                bank = take_aux(use)
                order = list(range(VPAIRS, NK)) + list(range(VPAIRS)) if (zero(c - 1), g) == (True, 0) else range(NK)
                for k in order:
                    n = PAIR_ROWS[k]
                    pe.wait_ge(*multiplied(c, g, k))
                    last = nc.tensor.matmul(bank[:], w1[0:n, k, :], pairs[0:n, g % 2, k, :],
                                            start=(k == order[0]), stop=(k == order[-1]))
                last.then_inc(aux_full, 1)

            def gram_product(c, tt):
                g, i = tt // GT, tt % GT
                if i == 0:
                    pe.wait_ge(diag_ready, c * NG + (g + 1))
                pe.wait_ge(x2_ready, c * TPC + (tt + 1))
                pe.wait_ge(gram_drained, c * TPC + (tt + 1))
                nc.tensor.matmul(gbank[:, 0:TB * FP], x2[:, i, :],
                                 x0diag[:, g % 2, i, :, :].rearrange("p r f -> p (r f)"),
                                 start=True, stop=True).then_inc(gram_ready, 1)

            def tile(c, tt):
                if tt % GT == 0:
                    pe.wait_ge(x1_ready, c * NG + (tt // GT + 1))
                for q, feats in enumerate(GROUPS):
                    before, back = (q - RING, 1) if q >= RING else (q - RING + NQ, 0)
                    if before in ACT_Q:
                        pe.wait_ge(prod_ready, c * (TPC * NA) + ((tt + back) * NA + ACT_Q.index(before) + 1))
                    else:
                        pe.wait_ge(acc_step, c * (TPC * NSTEPS) + ((tt + back) * NSTEPS + step_of(before) + 1))
                    n = len(feats) * M
                    out = ybank[q % RING][:, 0:n]
                    pos = slice(tt * 128, (tt + 1) * 128)
                    high = w2h[:, feats[0]:feats[-1] + 1, :].rearrange("p f m -> p (f m)")
                    low = w2l[:, feats[0]:feats[-1] + 1, :].rearrange("p f m -> p (f m)")
                    nc.tensor.matmul(out, x1h[:, pos], high, start=True, stop=False)
                    nc.tensor.matmul(out, x1h[:, pos], low, start=False, stop=False)
                    nc.tensor.matmul(out, x1l[:, pos], high, start=False, stop=True).then_inc(y_ready, 1)
                    if q == GRAM_AFTER and not (zero(c) and tt == 0):
                        gram_product(c, tt - 1)

            def layer3(c, g, use):
                pe.wait_ge(gram_drained, (c + 1) * TPC + 1)
                bank = take_aux(use)
                for f in range(F0):
                    last = nc.tensor.matmul(bank[:, 0:CH], w3[:, f, :], gram[:, f, :],
                                            start=(f == 0), stop=(f == F0 - 1))
                last.then_inc(aux_full, 1)

            def mlp1_start(c, use):
                bank = take_aux(use)
                for i in range(4):
                    cols = slice(i * 128, (i + 1) * 128)
                    nc.tensor.matmul(bank[:, cols], wt1[:, 0, cols],
                                     sum1[:, bass.ds(c, 1), :].rearrange("p c b -> p (c b)"), start=(i == 0), stop=False)
                    nc.tensor.matmul(bank[:, cols], wt1d[:, cols], denseT[:, bass.ds(c * CH, CH)],
                                     start=False, stop=False)

            def mlp1_rest(c, use, before):
                wait_use(before)
                bank = aux[bank_of(use)]
                for i in range(4):
                    cols = slice(i * 128, (i + 1) * 128)
                    nc.tensor.matmul(bank[:, cols], wt1[:, 1, cols], sum2[:], start=False, stop=False)
                    last = nc.tensor.matmul(bank[:, cols], wt1[:, 2, cols], s3[:], start=False, stop=(i == 3))
                last.then_inc(aux_full, 1)

            def mlp1(c, g, use, before):
                mlp1_start(c, use)
                mlp1_rest(c, use, before)

            def mlp2(c, g, use, before):
                wait_use(before)
                bank = take_aux(use)
                for i in range(2):
                    for k in range(4):
                        last = nc.tensor.matmul(bank[:, i * CH:(i + 1) * CH], wt2[:, k, i * 128:(i + 1) * 128],
                                                h1[:, k, :], start=(k == 0), stop=(k == 3))
                last.then_inc(aux_full, 1)

            def mlp3(c, g, use, before):
                wait_use(before)
                bank = take_aux(use)
                for k in range(2):
                    last = nc.tensor.matmul(bank[0:1, 0:CH], wt3[:, k:k + 1], h2[:, k, :],
                                            start=(k == 0), stop=(k == 1))
                last.then_inc(aux_full, 1)

            prep = {"x0T": x0_transposed, "x0P": x0_positions, "layer1": layer1}
            mlp = {"mlp1": mlp1, "mlp2": mlp2, "mlp3": mlp3}

            def keep_busy(matmuls):
                for _ in range(matmuls):
                    nc.tensor.matmul(gbank[:], w1[:, 0, :], w1[:, 0:4, :].rearrange("p k m -> p (k m)"),
                                     start=True, stop=True)

            pe.sem_inc(gram_ready, TPC)
            pe.wait_ge(w1_step, 2)
            pe.wait_ge(early_in, 16 * (F0 - LATE))
            keep_busy(4)
            pe.wait_ge(const_step, CONSTS)
            use = (0, 0)
            for what, g in PROLOGUE:
                if what == "x0P":
                    wait_positions(0, use)
                if (what, g) == ("layer1", 0):
                    keep_busy(3)
                prep[what](0, g, use)
                use = (use[0] + uses_of(what), 0)
            pe.wait_ge(w2h_ready, 1)
            pe.wait_ge(w2l_ready, 1)
            pe.wait_ge(w3_in, 16)
            pe.wait_ge(top_in, 16 * 7)

            def chunk(c, first, last):
                todo, _ = events(first, last)
                base = (USES0, 0) if first else (BASE, c)
                tail_use = None
                for tt in range(TPC):
                    for after, what, g, n in todo:
                        if after == tt and what == "x0P" and g < NG - 1:
                            wait_positions(c + 1, (base[0] + n, base[1]))
                    tile(c, tt)
                    for after, what, g, n in todo:
                        use = (base[0] + n, base[1])
                        if after != tt or what in COPIES:
                            continue
                        if what == "layer3":
                            layer3(c - 1, g, use)
                            tail_use = use
                        elif what in mlp:
                            mlp[what](c - 1, g, use, tail_use)
                            tail_use = use
                        elif what == "x0P" and g == NG - 1:
                            x0_positions(c, g, use)
                        else:
                            prep[what](c + 1, g, use)

            def finish(c):
                use = (BASE + events(False, True)[1], c)
                after = (use[0] + 1, c)
                mlp1_start(c, after)
                pe.wait_ge(gram_drained, c * TPC + TPC)
                keep_busy(1)
                gram_product(c, TPC - 1)
                layer3(c, 0, use)
                mlp1_rest(c, after, use)
                use = after
                for what in TAIL[2:]:
                    before, use = use, (use[0] + 1, c)
                    mlp[what](c, 0, use, before)

            chunk(0, True, False)
            with pe.Fori(1, NCH - 1) as c:
                chunk(c, False, False)
            chunk(NCH - 1, False, True)
            finish(NCH - 1)

        @block.scalar
        def _(act):
            act.dma_start(w2raw, t["f1"].rearrange("(f g) m -> g f m", g=M)).then_inc(w2_in, 16)
            act.dma_start(w3[:], t["f2"].rearrange("(f g) m -> g f m", g=M)).then_inc(w3_in, 16)
            act.dma_start(wt1[:], t["wt1"][0:384, :].rearrange("(k p) n -> p k n", p=128)).then_inc(top_in, 16)
            act.dma_start(wt1d[:], t["wt1"][384:400, :]).then_inc(top_in, 16)
            act.dma_start(wt2[:], t["wt2"].rearrange("(k p) n -> p k n", p=128)).then_inc(top_in, 16)
            act.dma_start(bt1[:], t["bt1"]).then_inc(top_in, 16)
            act.dma_start(bt2[:], t["bt2"]).then_inc(top_in, 16)
            act.dma_start(wt3[:], t["wt3"]).then_inc(top_in, 16)
            act.dma_start(denseT[:], t["denseT"]).then_inc(top_in, 16)
            act.sem_inc(prod_ready, NA)
            act.sem_inc(gram_drained, 1)
            act.wait_ge(w2_in, 16)
            nc.scalar.copy(w2h[:], w2raw).then_inc(w2h_ready, 1)

            def early_rows(c):
                act.wait_ge(early_in, (c + 1) * (16 * (F0 - LATE)))
                for j in range(SPT):
                    nc.scalar.copy(periods[:, j, EARLY_F, :], rows1[:, EARLY_F, :])
                nc.scalar.copy(rows[:, SPT * F0:PER, :], rows1[:, 0:PER - SPT * F0, :])

            def late_rows(c):
                act.wait_ge(late_in, (c + 1) * (16 * LATE))
                nc.scalar.copy(periods[:, :, LATE_F, :], rows1[:, LATE_F, :].unsqueeze(1)
                               .broadcast_to([CH, SPT, LATE, D])).then_inc(rows_copied, 1)

            def x0_transposed(c, g, use):
                if isinstance(c, int) and c == 1:
                    act.wait_ge(*multiplied(0, NG - 1, NK - 1))
                elif not isinstance(c, int):
                    act.wait_ge(*multiplied(c - 1, NG - 1, VPAIRS - 1))
                    act.wait_ge(*multiplied(c - 1, NG - 1, NK - 1))
                for u in range(X0T_USES):
                    now = (use[0] + u, use[1])
                    act.wait_ge(aux_full, filled(now))
                    nc.scalar.copy(x0per[:, :, 4 * u:4 * (u + 1)].rearrange("p b d -> p d b"),
                                   aux[bank_of(now)][0:PER, :].rearrange("p (d b) -> p d b", d=4)
                                   ).then_inc(aux_drained[bank_of(now)], 1)
                for now in ((use[0] + X0T_USES - 2, use[1]), (use[0] + X0T_USES - 1, use[1])):
                    act.wait_ge(aux_drained[bank_of(now)], taken_out(now))
                act.sem_inc(x0per_ready, 1)

            def x0_positions(c, g, use):
                if not zero(c):
                    act.wait_ge(x2_ready, c * TPC + ((g + 1) * GT - TPC))
                    act.wait_ge(diag_ready, c * NG + (g + 1 - NG))
                act.wait_ge(aux_full, filled(use))
                nc.scalar.copy(x0pos[:, g * GT:(g + 1) * GT, 0:F0],
                               aux[bank_of(use)][:, 0:GT * FP].rearrange("p (t f) -> p t f", f=FP)[:, :, 0:F0]
                               ).then_inc(aux_drained[bank_of(use)], 1)
                act.wait_ge(aux_drained[bank_of(use)], taken_out(use))
                act.sem_inc(x0pos_ready, 1)

            def layer1(c, g, use):
                act.wait_ge(aux_full, filled(use))
                nc.scalar.copy(x1h[:, 512 * g:512 * (g + 1)], aux[bank_of(use)][:]).then_inc(x1h_ready, 1)

            def gram_out(c, tt):
                act.wait_ge(gram_ready, c * TPC + tt + (TPC + 1))
                col = (TPC - 1) * TB if isinstance(tt, int) and tt < 0 else tt * TB
                nc.scalar.copy(gram[:, :, bass.ds(col, TB)].rearrange("p f r -> p r f"),
                               gbank[:, 0:TB * FP].rearrange("p (r f) -> p r f", f=FP)).then_inc(gram_drained, 1)

            def tile(c, tt, with_gram):
                for i, q in enumerate(ACT_Q):
                    ahead = NSTEPS if i >= PRODS else 0
                    act.wait_ge(acc_step, c * (TPC * NSTEPS) + tt * NSTEPS + (ahead + step_of(ACT_Q[(i - PRODS) % NA]) + 1))
                    act.wait_ge(y_ready, c * (TPC * NQ) + tt * NQ + (q + 1))
                    for j, f in enumerate(GROUPS[q]):
                        last = nc.scalar.activation(prod[:, i % PRODS, j * M:(j + 1) * M],
                                                    ybank[q % RING][:, j * M:(j + 1) * M], ACT.Copy,
                                                    scale=x0pos[:, bass.ds(tt, 1), f:f + 1].rearrange("p t f -> p (t f)"))
                    last.then_inc(prod_ready, 1)
                    if q == GRAM_AFTER and with_gram:
                        gram_out(c, tt - 1)

            def layer3(c, g, use):
                act.wait_ge(gram_drained, (c + 1) * TPC + 1)
                nc.scalar.copy(sum2[:], gram[:, F0, :])
                act.wait_ge(aux_full, filled(use))
                nc.scalar.copy(s3[:], aux[bank_of(use)][:, 0:CH]).then_inc(aux_drained[bank_of(use)], 1)

            def mlp1(c, g, use):
                act.wait_ge(aux_full, filled(use))
                for i in range(4):
                    last = nc.scalar.activation(h1[:, i, :], aux[bank_of(use)][:, i * CH:(i + 1) * CH], ACT.Relu,
                                                bias=bt1[:, i:i + 1])
                last.then_inc(aux_drained[bank_of(use)], 1)

            def mlp2(c, g, use):
                act.wait_ge(aux_full, filled(use))
                for i in range(2):
                    last = nc.scalar.activation(h2[:, i, :], aux[bank_of(use)][:, i * CH:(i + 1) * CH], ACT.Relu,
                                                bias=bt2[:, i:i + 1])
                last.then_inc(aux_drained[bank_of(use)], 1)

            def mlp3(c, g, use):
                act.wait_ge(aux_full, filled(use))
                nc.scalar.copy(y[:, bass.ds(c * CH, CH)],
                               aux[bank_of(use)][0:1, 0:CH]).then_inc(aux_drained[bank_of(use)], 1)

            prep = {"x0T": x0_transposed, "x0P": x0_positions, "layer1": layer1}
            copy_rows = dict(zip(COPIES, (early_rows, late_rows)))
            tail = {"layer3": layer3, "mlp1": mlp1, "mlp2": mlp2, "mlp3": mlp3}

            early_rows(0)
            late_rows(0)
            use = (0, 0)
            for what, g in PROLOGUE:
                prep[what](0, g, use)
                use = (use[0] + uses_of(what), 0)
            act.wait_ge(top_in, 16 * 7)

            def chunk(c, first, last, copies):
                todo, _ = events(first, last)
                base = (USES0, 0) if first else (BASE, c)
                tt = 0
                while tt < TPC:
                    if tt % GT == 0:
                        act.wait_ge(x0pos_ready, c * NG + (tt // GT + 1))
                    stop = min([after for after, *_ in todo if after >= tt] + [(tt // GT + 1) * GT - 1]) + 1
                    if stop - tt == 1 or tt == 0:
                        tile(c, tt, not (first and tt == 0))
                        stop = tt + 1
                    else:
                        with act.Fori(tt, stop) as i:
                            tile(c, i, True)
                    for after, what, g, n in todo:
                        use = (base[0] + n, base[1])
                        if after != stop - 1:
                            continue
                        if what in copy_rows:
                            if copies:
                                copy_rows[what](c + g)
                        elif what in tail:
                            tail[what](c - 1, g, use)
                        else:
                            prep[what](c if (what, g) == ("x0P", NG - 1) else c + 1, g, use)
                    tt = stop

            def finish(c):
                gram_out(c, TPC - 1)
                use = (BASE + events(False, True)[1], c)
                for what in TAIL:
                    tail[what](c, 0, use)
                    use = (use[0] + 1, c)

            chunk(0, True, False, True)
            with act.Fori(1, NCH - 2) as c:
                chunk(c, False, False, True)
            chunk(NCH - 2, False, False, False)
            chunk(NCH - 1, False, True, False)
            finish(NCH - 1)

        @block.vector
        def _(dve):
            dve.sem_inc(acc_step, NSTEPS)
            nc.vector.memset(w1t[0:F0, 0, :], 0.0).then_inc(w1_step, 1)
            dve.wait_ge(w1_step, 1)
            dve.wait_ge(w1_in, 16 * 3)
            nc.vector.tensor_tensor(w1[:], w1[:], w1t[:], ALU.add).then_inc(w1_step, 1)
            dve.wait_ge(w2h_ready, 1)
            nc.vector.tensor_tensor(w2l[:], w2raw, w2h[:].bitcast(fp32), ALU.subtract).then_inc(w2l_ready, 1)

            def multiply_pairs(c, g, tiles):
                for k in range(tiles):
                    n = PAIR_ROWS[k]
                    if k == 0:
                        dve.wait_ge(factor_in[g % 2], slot_count(c, g, SPT))
                        shifted = x0per[0:n, g * GB:(g + 1) * GB, :].rearrange("p b d -> p (b d)")
                    else:
                        dve.wait_ge(shifted_in[g % 2][k], slot_count(c, g, 1))
                        shifted = pairs[0:n, g % 2, k, :]
                    nc.vector.tensor_tensor(pairs[0:n, g % 2, k, :], shifted, factor[0:n, g % 2, :],
                                            ALU.mult).then_inc(vpairs_ready, 1)

            def layer1(c, g, use):
                cols = slice(512 * g, 512 * (g + 1))
                dve.wait_ge(x1h_ready, c * NG + (g + 1))
                bank = aux[bank_of(use)]
                nc.vector.tensor_tensor(x1l[:, cols], bank[:], x1h[:, cols].bitcast(fp32),
                                        ALU.subtract).then_inc(x1_ready, 1)
                nc.vector.tensor_reduce(sum1[:, bass.ds(c, 1), g * GB:(g + 1) * GB].rearrange("p c b -> p (c b)"),
                                        bank[:].rearrange("p (b d) -> p b d", d=D), AX.X,
                                        ALU.add).then_inc(aux_drained[bank_of(use)], 1)

            multiply_pairs(0, 0, NK)
            for g in range(NG):
                if g + 1 < NG:
                    multiply_pairs(0, g + 1, NK)
                layer1(0, g, layer1_use(0, g))

            def tiles(c, g, start, stop):
                with dve.Fori(start // 2, stop // 2) as pair:
                    for slot in range(2):
                        tile(c, g, pair * 2 + slot, slot)

            def tile(c, g, tt, slot):
                done = c * (TPC * NSTEPS) + (tt + 1) * NSTEPS
                groups = c * (TPC * NQ) + tt * NQ
                products = c * (TPC * NA) + (tt + 1) * NA

                dve.wait_ge(x0pos_ready, c * NG + (g + 1))

                def product(q):
                    i = ACT_Q.index(q)
                    dve.wait_ge(prod_ready, products + (i + 1))
                    return prod[:, i % PRODS, :]

                dve.wait_ge(joined, c * TPC + tt + 1)
                for i, (kind, used) in enumerate(STEPS):
                    if step_before(i):
                        dve.wait_ge(acc_step, done + step_before(i))
                    if kind == "scale":
                        q = used[0]
                        start = product(used[1]) if len(used) > 1 else scaled[:, slot, :]
                        dve.wait_ge(y_ready, groups + (q + 1))
                        for j, f in enumerate(GROUPS[q]):
                            cols = slice(j * M, (j + 1) * M)
                            last = nc.vector.scalar_tensor_tensor(
                                out=scaled[:, slot, cols], in0=ybank[q % RING][:, cols],
                                scalar=x0pos[:, bass.ds(tt, 1), f:f + 1].rearrange("p t f -> p (t f)"),
                                in1=start[:, cols], op0=ALU.mult, op1=ALU.add)
                    else:
                        terms = [product(q) for q in used]
                        last = nc.vector.tensor_tensor(
                            added[:, slot, :], terms[0], terms[1] if len(terms) > 1 else added[:, slot, :], ALU.add)
                    last.then_inc(acc_step, 1)

            def chunk(c, first, last):
                after = {tile + 1: g for tile, what, g, _ in events(first, last)[0] if what == "layer1"}
                multiply_after = FIRST_VPAIRS_AFTER if first else VPAIRS_AFTER
                start = 0
                for stop in range(2, TPC + 1, 2):
                    if stop % GT == 0 or stop in after or stop - 1 in multiply_after:
                        tiles(c, start // GT, start, stop)
                        start = stop
                    if stop - 1 in multiply_after and not last:
                        for g in multiply_after[stop - 1]:
                            multiply_pairs(c + 1, g, VPAIRS)
                    if stop in after:
                        layer1(c + 1, after[stop], layer1_use(c + 1, after[stop]))

            def fold_last():
                slot, tiles = (TPC - 1) % 2, NCH * TPC
                dve.wait_ge(acc_step, (tiles + 1) * NSTEPS)
                nc.vector.tensor_tensor(scaled[:, slot, :], scaled[:, slot, :], added[:, slot, :],
                                        ALU.add).then_inc(vfolded, 1)
                dve.wait_ge(vfolded, 1)
                nc.vector.tensor_tensor(scaled[:, slot, 0:256], scaled[:, slot, 0:256], scaled[:, slot, 256:512],
                                        ALU.add).then_inc(vfolded, 1)
                dve.wait_ge(vfolded, 2)
                dve.wait_ge(gram_ready, tiles - GT + TPC)
                dve.wait_ge(x2_ready, tiles - 1)
                nc.vector.tensor_tensor(x2[:, (TPC - 1) % GT, :], scaled[:, slot, 0:128], scaled[:, slot, 128:256],
                                        ALU.add).then_inc(x2_ready, 1)

            chunk(0, True, False)
            with dve.Fori(1, NCH - 1) as c:
                chunk(c, False, False)
            chunk(NCH - 1, False, True)
            fold_last()


def pair_rows():
    pairs = [[((i - NK * j) % F0, (i + k) % F0) for k in range(NK)] for j in range(SPT) for i in range(F0)]
    return [[f * F0 + g for f, g in p] for p in pairs], [[g * F0 + f for f, g in p] for p in pairs]


def kernel(**inputs):
    import numpy as np
    import concourse.bacc as bacc
    from concourse.bass_utils import run_bass_kernel_spmd

    nc = bacc.Bacc("TRN2", target_bir_lowering=False, num_devices=1)
    arrays = {}

    def dram(name, a):
        a = np.ascontiguousarray(a)
        name = f"in_{name}"
        arrays[name] = a
        return nc.dram_tensor(name, a.shape, mybir.dt.from_np(a.dtype), kind="ExternalInput").ap()

    first, second = pair_rows()
    f0 = np.asarray(inputs["L0_rec_f0"])
    t = {
        "ids": dram("ids", inputs["ids"]),
        "tables": [dram(f"table{f}", inputs[f"tbl_{f}"]) for f in range(F0)],
        "w1a": dram("w1a", f0[first]),
        "w1b": dram("w1b", f0[second]),
        "f1": dram("f1", inputs["L0_rec_f1"]),
        "f2": dram("f2", inputs["L0_rec_f2"]),
        "denseT": dram("denseT", np.asarray(inputs["dense_ctx"]).T),
        "wt1": dram("wt1", inputs["W_top1"]),
        "wt2": dram("wt2", inputs["W_top2"]),
        "bt1": dram("bt1", np.asarray(inputs["b_top1"]).reshape(4, 128).T),
        "bt2": dram("bt2", np.asarray(inputs["b_top2"]).reshape(2, 128).T),
        "wt3": dram("wt3", np.asarray(inputs["W_top3"]).reshape(2, 128).T),
        "out": nc.dram_tensor("out", (B, 1), mybir.dt.float32, kind="ExternalOutput").ap(),
    }
    build(nc, t)
    r = run_bass_kernel_spmd(nc, [arrays], core_ids=[0])
    return r.results[0]["out"]
```
